# Optimizing a Trainium2 kernel written in Bass

```python
import numpy as np
import jax
import jax.numpy as jnp

def _softmax(x, axis=-1):
    return jax.nn.softmax(x, axis=axis)

def _gelu(x):
    return jax.nn.gelu(x, approximate=True)

def _silu(x):
    return jax.nn.silu(x)

def _sigmoid(x):
    return jax.nn.sigmoid(x)

def _layernorm(x, axis=-1, eps=1e-05):
    m = jnp.mean(x, axis=axis, keepdims=True)
    v = jnp.var(x, axis=axis, keepdims=True)
    return (x - m) / jnp.sqrt(v + eps)

def _scatter_add(tgt, idx, src, axis=0):
    return tgt.at[idx].add(src)

def _segment_sum(src, seg, n):
    return jax.ops.segment_sum(src, seg, n)
kernel_name = 'mk_adj_preln_d4_adj_r2_af898b'

def setup_inputs(seed: int=0):
    np.random.seed(seed)
    _w = jnp.asarray

    def _rec_inputs():
        import jax
        import jax.numpy as jnp
        _gk = jax.random.key(seed)
        x = -0.0005207 + 1.001 * jax.random.normal(jax.random.fold_in(_gk, 1), (4096, 256), jnp.float32)
        _a = jax.random.bernoulli(jax.random.fold_in(_gk, 2), 0.00390625, (4096, 4096))
        _a = jnp.logical_or(_a, jnp.eye(4096, dtype=bool))
        _af = _a.astype(jnp.float32)
        _af = _af * jax.random.uniform(jax.random.fold_in(_gk, 3), (4096, 4096), jnp.float32, 0.05, 1)
        adj = _af
        return (x, adj)
    x, adj = _rec_inputs()

    def _L0_gnn_setup():
        import jax, jax.numpy as jnp
        import numpy as np
        N = 2048
        D_IN = 256
        D_OUT = 256
        key = jax.random.key(seed)
        k1, k2, k3 = jax.random.split(key, 3)
        X = jax.random.normal(k1, (N, D_IN), dtype=jnp.float32)
        A = jax.random.uniform(k2, (N, N), dtype=jnp.float32)
        W = jax.random.normal(k3, (D_OUT, D_IN), dtype=jnp.float32) * (1.0 / np.sqrt(D_IN))
        return {'X': X, 'A': A, 'W': W}
    _L0_gnn_all = _L0_gnn_setup()
    _L0_gnn_in = {k: v for k, v in _L0_gnn_all.items() if k in ('W',)}
    del _L0_gnn_all

    def _L1_gnn_setup():
        import jax, jax.numpy as jnp
        import numpy as np
        N = 4096
        DIN = 256
        DOUT = 256
        TAU = 1.0
        EPS = 1e-08
        NORM_EPS = 1e-08
        key = jax.random.key(seed)
        k1, k2, k3 = jax.random.split(key, 3)
        x = jax.random.normal(k1, (N, DIN), dtype=jnp.float32)
        adj = jax.random.uniform(k2, (N, N), dtype=jnp.float32)
        limit = float(np.sqrt(6.0 / (DIN + DOUT)))
        weight = jax.random.uniform(k3, (DIN, DOUT), dtype=jnp.float32, minval=-limit, maxval=limit)
        bias = jnp.zeros((DOUT,), dtype=jnp.float32)
        return {'x': x, 'adj': adj, 'weight': weight, 'bias': bias}
    _L1_gnn_all = _L1_gnn_setup()
    _L1_gnn_in = {k: v for k, v in _L1_gnn_all.items() if k in ('weight', 'bias')}
    del _L1_gnn_all

    def _L2_gnn_setup():
        import jax, jax.numpy as jnp
        import numpy as np
        N = 4096
        DIN = 256
        DOUT = 256
        key = jax.random.key(seed)
        k1, k2, k3 = jax.random.split(key, 3)
        x = jax.random.normal(k1, (N, DIN), dtype=jnp.float32)
        adj = jax.random.uniform(k2, (N, N), dtype=jnp.float32)
        W = jax.random.normal(k3, (DIN, DOUT), dtype=jnp.float32) * (1.0 / np.sqrt(DIN))
        b = jnp.zeros((DOUT,), dtype=jnp.float32)
        return {'x': x, 'adj': adj, 'W': W, 'b': b}
    _L2_gnn_all = _L2_gnn_setup()
    _L2_gnn_in = {k: v for k, v in _L2_gnn_all.items() if k in ('W', 'b')}
    del _L2_gnn_all

    def _L3_gnn_setup():
        import jax, jax.numpy as jnp
        import numpy as np
        N, NFEAT, NHID = (8192, 256, 256)

        def _gc_layer(x, adj, W):
            support = adj @ x
            h = jnp.concatenate([x, support], axis=1)
            return h @ W
        key = jax.random.key(seed)
        k1, k2, k3, k4 = jax.random.split(key, 4)
        x = jax.random.normal(k1, (N, NFEAT), dtype=jnp.float32)
        adj = jax.random.uniform(k2, (N, N), dtype=jnp.float32)
        stdv1 = 1.0 / np.sqrt(NHID)
        W1 = jax.random.uniform(k3, (2 * NFEAT, NHID), dtype=jnp.float32, minval=-stdv1, maxval=stdv1)
        W2 = jax.random.uniform(k4, (2 * NHID, NHID), dtype=jnp.float32, minval=-stdv1, maxval=stdv1)
        return {'x': x, 'adj': adj, 'W1': W1, 'W2': W2}
    _L3_gnn_all = _L3_gnn_setup()
    _L3_gnn_in = {k: v for k, v in _L3_gnn_all.items() if k in ('W1', 'W2')}
    del _L3_gnn_all
    return {'x': x, 'adj': adj, 'L0_gnn_W': _L0_gnn_in['W'], 'L1_gnn_weight': _L1_gnn_in['weight'], 'L1_gnn_bias': _L1_gnn_in['bias'], 'L2_gnn_W': _L2_gnn_in['W'], 'L2_gnn_b': _L2_gnn_in['b'], 'L3_gnn_W1': _L3_gnn_in['W1'], 'L3_gnn_W2': _L3_gnn_in['W2']}

def reference(x, adj, L0_gnn_W, L1_gnn_weight, L1_gnn_bias, L2_gnn_W, L2_gnn_b, L3_gnn_W1, L3_gnn_W2):
    import jax
    import jax.numpy as jnp

    def _L0_gnn_ref(X, A, W):
        import jax, jax.numpy as jnp
        import numpy as np
        N = 2048
        D_IN = 256
        D_OUT = 256
        A2 = A + jnp.eye(A.shape[0], dtype=A.dtype)
        dscale = jnp.diagonal(A2) ** (-0.5)
        temp = A2 @ X @ W.T
        A_norm = dscale[:, None] * A2 * dscale[None, :]
        return jax.nn.relu(A_norm @ temp)

    def _L1_gnn_ref(x, adj, weight, bias):
        import jax, jax.numpy as jnp
        import numpy as np
        N = 4096
        DIN = 256
        DOUT = 256
        TAU = 1.0
        EPS = 1e-08
        NORM_EPS = 1e-08
        h = x @ weight
        norm = jnp.linalg.norm(h, axis=1, keepdims=True)
        h_norm = h / jnp.maximum(norm, NORM_EPS)
        sim = h_norm @ h_norm.T
        attn_logits = sim / TAU + jnp.log(adj + EPS)
        attn = jax.nn.softmax(attn_logits, axis=1)
        out = attn @ h + bias
        return out

    def _L2_gnn_ref(x, adj, W, b):
        import jax, jax.numpy as jnp
        import numpy as np
        N = 4096
        DIN = 256
        DOUT = 256
        rowsum = adj.sum(axis=1)
        d_inv_sqrt = jnp.where(rowsum > 0, rowsum ** (-0.5), 0.0)
        normalized_adj = d_inv_sqrt[:, None] * adj * d_inv_sqrt[None, :]
        support = normalized_adj @ x
        out = support @ W + b
        return jax.nn.relu(out)

    def _L3_gnn_ref(x, adj, W1, W2):
        import jax, jax.numpy as jnp
        import numpy as np
        N, NFEAT, NHID = (8192, 256, 256)

        def _gc_layer(x, adj, W):
            support = adj @ x
            h = jnp.concatenate([x, support], axis=1)
            return h @ W
        h = jax.nn.relu(_gc_layer(x, adj, W1))
        h = jax.nn.relu(_gc_layer(h, adj, W2))
        return h
    h = jnp.maximum(_layernorm(x, axis=-1), 0.0)
    x = x + _L0_gnn_ref(h, adj, L0_gnn_W)
    h = jnp.maximum(_layernorm(x, axis=-1), 0.0)
    x = x + _L1_gnn_ref(h, adj, L1_gnn_weight, L1_gnn_bias)
    h = jnp.maximum(_layernorm(x, axis=-1), 0.0)
    x = x + _L2_gnn_ref(h, adj, L2_gnn_W, L2_gnn_b)
    h = jnp.maximum(_layernorm(x, axis=-1), 0.0)
    x = x + _L3_gnn_ref(h, adj, L3_gnn_W1, L3_gnn_W2)
    return x

_drawn_inputs = setup_inputs


def setup_inputs(seed=0):
    import zlib

    import numpy as np

    out = dict(_drawn_inputs(seed))
    spreads = {'L1_gnn_bias': (0.0, 0.8), 'L2_gnn_b': (0.0, 2.0)}
    factors = {}
    for name, (base, spread) in spreads.items():
        noise = np.random.default_rng([zlib.crc32(name.encode()), seed]).standard_normal(out[name].shape)
        drawn = base * np.exp(spread * noise) if base else spread * noise
        out[name] = jnp.asarray(drawn.astype(out[name].dtype))
    for name, factor in factors.items():
        out[name] = (out[name] * factor).astype(out[name].dtype)
    return out
```

```python
from contextlib import ExitStack

import concourse.bass as bass
import numpy as np
from concourse import mybir

N = 4096
F = 256
P = 128
NB = N // P
GB = 4
NG = NB // GB
NC = NB // GB
GR = GB * P
FB = F // P
MW = 2 * F + 2
LO = F + 2
LN_EPS = 1e-5
ADJ_EPS = 1e-8
NORM_EPS = 1e-8
TINY = 1.2e-38
ADJ_SCALE = 256.0
W_SCALE = 64.0
P_SCALE = 4096.0
GN_SCALE = 64.0
LEAD = 3
PRE = -1
ATT = 2

SMALL_N = {PRE: F, 1: F, 2: F, 3: 2 * F, 4: 2 * F}


def build(nc, x, adj_t, w0, wg, bias_g, w2, bias_2, w3a, w3b, out):
    f32, f16 = mybir.dt.float32, mybir.dt.float16
    ALU, ACT = mybir.AluOpType, mybir.ActivationFunctionType

    ctx = ExitStack()
    with ctx:
        def sb(name, shape, dt):
            return ctx.enter_context(nc.sbuf_tensor(name, shape, dt))

        def pb(name, shape, dt):
            return ctx.enter_context(nc.psum_tensor(name, shape, dt))

        def sem(name):
            return ctx.enter_context(nc.semaphore(name))

        xres = sb("xres", [P, NB, F], f32)
        mov = [sb(f"mov{i}", [P, NB, MW], f16) for i in range(2)]
        shared = sb("shared", [P, 2 * FB * N // 2], f32)
        gnT = shared[:, :].bitcast(f16).rearrange("p (q n) -> p q n", q=2 * FB)
        direct = shared[:, :].rearrange("p (b n) -> p b n", n=F)
        wcols = [F, F, F, 2 * F, 2 * F]
        wofs = [sum(wcols[:i]) * FB for i in range(6)]
        wraw = [shared[:, wofs[i]:wofs[i + 1]].rearrange("p (f n) -> p f n", f=FB) for i in range(5)]
        wsp = sb("wsp", [P, 2, wofs[5]], f16)
        wpart = [[wsp[:, s, wofs[i]:wofs[i + 1]].rearrange("p (f n) -> p f n", f=FB) for s in range(2)]
                 for i in range(5)]
        weights_of = {PRE: wpart[0], 1: wpart[1], 2: wpart[2], 3: wpart[3], 4: wpart[4]}
        adj = sb("adj", [P, 2, GB, GR], f32)
        ahi = sb("ahi", [P, 2, GB, GR], f16)
        alo = sb("alo", [P, 2, GB, GR], f16)
        expo = sb("expo", [P, GB, GR], f32)
        ev = sb("ev", [P, GB, F + 1], f32)
        o = sb("o", [P, GB, F], f32)
        hsp = sb("hsp", [P, 2, GB, F], f16)
        hT = sb("hT", [P, 2 * FB, GR], f16)
        bg = sb("bg", [P, F], f32)
        b2 = sb("b2", [P, F], f32)
        ident = sb("ident", [P, P], f16)
        diag = sb("diag", [P, NB], f32)
        d = sb("d", [P, NB], f32)
        dinv = sb("dinv", [P, NB], f32)
        dinv_w = sb("dinv_w", [P, NB], f32)
        neghalf = sb("neghalf", [P, NB], f32)
        stats = sb("stats", [P, GB, 6], f32)
        mv = sb("mv", [P, GB, 2], f32)
        vare = sb("vare", [P, GB], f32)
        rstd = sb("rstd", [P, GB], f32)
        rowc = sb("rowc", [P, GB], f32)
        rowm = sb("rowm", [P, GB], f32)
        rowp = sb("rowp", [P, GB], f32)
        rden = sb("rden", [P, GB], f32)
        ssq = sb("ssq", [P, GB], f32)
        ssqc = sb("ssqc", [P, GB], f32)
        rnorm = sb("rnorm", [P, GB], f32)
        junk = sb("junk", [P, GB, F], f16)

        acc = pb("acc", [P, GB, GR], f32)
        psT = pb("psT", [P, 2 * FB, 2 * P], f16)
        psW = pb("psW", [P, 2 * F], f32)
        psS = pb("psS", [P, 2, GR], f32)

        w_loaded = sem("w_loaded")
        b_loaded = sem("b_loaded")
        diag_loaded = sem("diag_loaded")
        x_loaded = [sem(f"x_loaded{q}") for q in range(NG)]
        adj_loaded = [sem(f"adj_loaded{s}") for s in range(2)]
        stored = sem("stored")
        const_ready = sem("const_ready")
        ident_zero = sem("ident_zero")
        ones_ready = sem("ones_ready")
        w_hi = sem("w_hi")
        w_ready = sem("w_ready")
        diag_one = sem("diag_one")
        d_ready = sem("d_ready")
        split_hi = sem("split_hi")
        split_ready = sem("split_ready")
        chunk_done = sem("chunk_done")
        sim_ready = sem("sim_ready")
        exp_ready = sem("exp_ready")
        num_ready = sem("num_ready")
        num_hi = sem("num_hi")
        num_split = sem("num_split")
        block_done = sem("block_done")
        acc_ready = sem("acc_ready")
        ev_ready = sem("ev_ready")
        sum_hi = sem("sum_hi")
        sum_ready = sem("sum_ready")
        row_ready = sem("row_ready")
        rowp_ready = sem("rowp_ready")
        dinv_ready = sem("dinv_ready")
        den_ready = sem("den_ready")
        scaled = sem("scaled")
        preact = sem("preact")
        x_ready = sem("x_ready")
        stats_ready = sem("stats_ready")
        passed = sem("passed")
        mv_ready = sem("mv_ready")
        var_ready = sem("var_ready")
        rstd_ready = sem("rstd_ready")
        normed = sem("normed")
        h_hi = sem("h_hi")
        h_ready = sem("h_ready")
        h_turned = sem("h_turned")
        hT_ready = sem("hT_ready")
        small_ready = sem("small_ready")
        direct_ready = sem("direct_ready")
        mov_hi = sem("mov_hi")
        mov_ready = sem("mov_ready")
        ssq_ready = sem("ssq_ready")
        ssqc_ready = sem("ssqc_ready")
        rnorm_ready = sem("rnorm_ready")
        gn_hi = sem("gn_hi")
        gn_ready = sem("gn_ready")
        gn_turned = sem("gn_turned")
        gnT_ready = sem("gnT_ready")

        ALL = [0, 1, 2, 3, 4, 5]
        NORM = [PRE, 1, 2, 3]
        SMALL = [PRE, 1, 2, 3, 4]
        SELF = [0, 1]
        RES = [1, 2, 3, 5]
        SCALED = [1, 2, 3]
        DIRECT = [3, 4]
        MOVE = [PRE, 0, 1, 2, 3, 4]

        def at(passes, p, g, per=1, k=1):
            return (g + NG * passes.index(p)) * per + k

        PLAIN = [0, 1, 3, 4, 5]

        def chunk_no(p, g, c):
            return (g + NG * PLAIN.index(p)) * NC + c

        def all_chunk_no(p, g, c):
            return (g + NG * p) * NC + c

        block = ctx.enter_context(nc.Block())

        @block.sync
        def _(sp):
            def load(p, g, c, first=False):
                if not first:
                    q, h, e = (p, g, c - 2) if c >= 2 else ((p, g - 1, c + 6) if not isinstance(g, int) or g > 0
                                                            else (p - 1, NG - 1, c + 6))
                    if q == ATT:
                        sp.wait_ge(num_ready, h * NB + GB * (e + 1))
                    else:
                        sp.wait_ge(split_ready, chunk_no(q, h, e) + 1)
                row = (g * NC + c) * P if isinstance(g, int) else g * (NC * P) + c * P
                sp.dma_start(adj[:, c % 2, :, :].rearrange("p b n -> p (b n)"), adj_t[bass.ds(row, P), :])\
                    .then_inc(adj_loaded[c % 2], 16)

            def store(g):
                sp.wait_ge(x_ready, at(RES, 5, g))
                sp.dma_start(out[bass.ds(g * GR, GR), :].rearrange("(b p) n -> p b n", p=P),
                             xres[:, bass.ds(g * GB, GB), :]).then_inc(stored, 16)

            def group(p, g, first=False):
                for c in range(NC):
                    load(p, g, c, first and c < 2)
                    if p == 5 and c == 5 and not isinstance(g, int):
                        store(g - 1)

            for p in range(6):
                group(p, 0, first=p == 0)
                with sp.Fori(1, NG) as g:
                    group(p, g)
            store(NG - 1)
            sp.wait_ge(stored, 16 * NG)

        @block.gpsimd
        def _(pool):
            nc.gpsimd.memset(ident[:, :], 0.0).then_inc(ident_zero, 1)
            nc.gpsimd.memset(neghalf[:, :], -0.5).then_inc(const_ready, 1)
            pool.wait_ge(ident_zero, 1)
            nc.gpsimd.affine_select(out=ident[:, :], in_=ident[:, :], compare_op=ALU.not_equal, fill=1.0,
                                    base=0, pattern=[[-1, P]], channel_multiplier=1).then_inc(const_ready, 1)
            pool.wait_ge(const_ready, 2)
            pool.wait_ge(diag_one, 1)
            nc.gpsimd.tensor_tensor(out=d[:, :], in0=diag[:, :], in1=neghalf[:, :], op=ALU.pow).then_inc(d_ready, 1)

            def rstd_of(p, g):
                pool.wait_ge(var_ready, at(NORM, p, g))
                nc.gpsimd.tensor_tensor(out=rstd[:, :], in0=vare[:, :], in1=neghalf[:, 0:GB], op=ALU.pow)\
                    .then_inc(rstd_ready, 1)

            def tail(p, g):
                if p == 0:
                    pool.wait_ge(row_ready, at([0], p, g, 2, 2))
                    nc.gpsimd.tensor_tensor(out=rowp[:, :], in0=rowc[:, :], in1=neghalf[:, 0:GB], op=ALU.pow)\
                        .then_inc(rowp_ready, 1)
                if p in NORM:
                    rstd_of(p, g)
                if p == 1:
                    for r in range(2):
                        pool.wait_ge(ssqc_ready, at([1], p, g, 2, r + 1))
                        nc.gpsimd.tensor_tensor(out=rnorm[:, 2 * r:2 * r + 2], in0=ssqc[:, 2 * r:2 * r + 2],
                                                in1=neghalf[:, 0:2], op=ALU.pow).then_inc(rnorm_ready, 1)

            for p in [PRE, 0, 1, 2, 3]:
                with pool.Fori(0, NG) as g:
                    tail(p, g)

        @block.tensor
        def _(pe):
            def product(p, g, c, b, k, first, last):
                jb = GB * c + k
                m = mov[p % 2]
                n = F + 1 if p in (0, ATT) else F
                cols = slice(b * P, (b + 1) * P)
                hi, lo = ahi[:, c % 2, k, cols], alo[:, c % 2, k, cols]
                nc.tensor.matmul(acc[:, b, 0:n], hi, m[:, jb, 0:n], start=first, stop=False)
                nc.tensor.matmul(acc[:, b, 0:F], hi, m[:, jb, LO:LO + F], start=False, stop=False)
                return nc.tensor.matmul(acc[:, b, 0:n], lo, m[:, jb, 0:n], start=False, stop=last)

            def bank_free(p, g, b):
                if isinstance(g, int) and g == 0:
                    if p > 0:
                        pe.wait_ge(ev_ready, at(ALL, p - 1, NG - 1, GB, b + 1))
                else:
                    pe.wait_ge(ev_ready, at(ALL, p, g - 1, GB, b + 1))

            def turn(p, g, r):
                pe.wait_ge(h_ready, at(SMALL, p, g))
                if r == 1:
                    pe.wait_ge(hT_ready, at(SMALL, p, g, 2, 1))
                elif not isinstance(g, int) or g > 0:
                    pe.wait_ge(hT_ready, at(SMALL, p, g - 1, 2, 2))
                    if p == 1:
                        pe.wait_ge(gnT_ready, at([1], p, g - 1, 2, 2))
                elif p > PRE:
                    before = SMALL[SMALL.index(p) - 1]
                    pe.wait_ge(hT_ready, at(SMALL, before, NG - 1, 2, 2))
                    if p == 2:
                        pe.wait_ge(gnT_ready, at([1], 1, NG - 1, 2, 2))
                transposes(r).then_inc(h_turned, 1)

            def transposes(r):
                for q in range(2 * FB):
                    for b in range(2):
                        last = nc.tensor.transpose(psT[:, q, b * P:(b + 1) * P],
                                                   hsp[:, q // FB, 2 * r + b, (q % FB) * P:(q % FB + 1) * P],
                                                   ident[:, :])
                return last

            def small(p, g, r):
                n = SMALL_N[p]
                whi, wlo = weights_of[p]
                pe.wait_ge(hT_ready, at(SMALL, p, g, 2, r + 1))
                if r == 1:
                    pe.wait_ge(mov_ready, at(MOVE, p, g, GB, 2))
                    if p == 1:
                        pe.wait_ge(gn_ready, at([1], p, g, GB, 2))
                elif not isinstance(g, int) or g > 0:
                    pe.wait_ge(mov_ready, at(MOVE, p, g - 1, GB, 4))
                    if p == 1:
                        pe.wait_ge(gn_ready, at([1], p, g - 1, GB, 4))
                elif p > PRE:
                    pe.wait_ge(mov_ready, at(MOVE, p - 1, NG - 1, GB, 4))
                    if p == 2:
                        pe.wait_ge(gn_ready, at([1], 1, NG - 1, GB, 4))
                for b in range(2):
                    rows = slice((2 * r + b) * P, (2 * r + b + 1) * P)
                    to = psW[:, b * F:b * F + n] if n == F else (psW[:, :] if b == 0 else psS[:, 0, :])
                    for f in range(FB):
                        nc.tensor.matmul(to, hT[:, f, rows], whi[:, f, :], start=f == 0, stop=False)
                        nc.tensor.matmul(to, hT[:, f, rows], wlo[:, f, :], start=False, stop=False)
                        last = nc.tensor.matmul(to, hT[:, FB + f, rows], whi[:, f, :], start=False,
                                                stop=f == FB - 1)
                last.then_inc(small_ready, 1)

            def turn_gn(p, g, r):
                pe.wait_ge(gn_ready, at([1], p, g, GB, 2 * r + 2))
                if r == 0:
                    pe.wait_ge(hT_ready, at(SMALL, p, g, 2, 2))
                else:
                    pe.wait_ge(gnT_ready, at([1], p, g, 2, 1))
                transposes(r).then_inc(gn_turned, 1)

            def step(name, p, g):
                if name == "T0":
                    turn(p, g, 0)
                elif name == "W0T1":
                    small(p, g, 0)
                    turn(p, g, 1)
                elif name == "W1":
                    small(p, g, 1)
                elif p == 1:
                    turn_gn(p, g, int(name[1]))

            PLACES = {(3, 0): "T0", (4, 0): "W0T1", (5, 0): "W1", (6, 0): "G0", (6, 2): "G1"}
            ATT_PLACES = {8: "T0", 10: "W0T1", 13: "W1", 16: "G0", 18: "G1"}

            def moving_there(p, g, c):
                if isinstance(g, int) and g == 0:
                    pe.wait_ge(mov_ready, at(MOVE, p - 1, c, GB, 4))

            def group(p, g, tp, tg):
                for c in range(NC):
                    pe.wait_ge(split_ready, chunk_no(p, g, c) + 1)
                    moving_there(p, g, c)
                    for b in range(GB):
                        if c == 0:
                            bank_free(p, g, b)
                        for k in range(GB):
                            last = product(p, g, c, b, k, c == 0 and k == 0, c == NC - 1 and k == GB - 1)
                        if c == NC - 1:
                            last.then_inc(acc_ready, 1)
                        elif b == GB - 1:
                            last.then_inc(chunk_done, 1)
                        if tp in SMALL and tp != PRE and (c, b) in PLACES:
                            step(PLACES[c, b], tp, tg)
                        if tp == PRE and c < NC - 1 and b < 3:
                            step(["T0", "W0T1", "W1"][b], PRE, c + 1)

            def cosines(g, c, k, n):
                if isinstance(g, int) and g == 0 and k == 0:
                    pe.wait_ge(gnT_ready, at([1], 1, c, 2, 2))
                if not (isinstance(n, int) and n < 2):
                    pe.wait_ge(exp_ready, n - 1)
                jb = GB * c + k
                rows = bass.ds(g * GR, GR)
                for f in range(FB):
                    hi, lo = gnT[:, f, jb * P:(jb + 1) * P], gnT[:, FB + f, jb * P:(jb + 1) * P]
                    mhi, mlo = gnT[:, f, rows], gnT[:, FB + f, rows]
                    nc.tensor.matmul(psS[:, k % 2, :], hi, mhi, start=f == 0, stop=False)
                    nc.tensor.matmul(psS[:, k % 2, :], hi, mlo, start=False, stop=False)
                    last = nc.tensor.matmul(psS[:, k % 2, :], lo, mhi, start=False, stop=f == FB - 1)
                last.then_inc(sim_ready, 1)

            def att_group(g, tp, tg, last_group=False):
                for j in range(NB):
                    ahead = j + LEAD
                    if ahead < NB:
                        cosines(g, ahead // GB, ahead % GB, g * NB + ahead)
                    elif not last_group:
                        cosines(g + 1, 0, ahead - NB, g * NB + ahead)
                    pe.wait_ge(num_split, g * NB + j + 1)
                    if j % GB == 0:
                        moving_there(ATT, g, j // GB)
                    for b in range(GB):
                        if j == 0:
                            bank_free(ATT, g, b)
                        last = product(ATT, g, j // GB, b, j % GB, j == 0, j == NB - 1)
                        if j == NB - 1:
                            last.then_inc(acc_ready, 1)
                        elif b == GB - 1:
                            last.then_inc(block_done, 1)
                    if j in ATT_PLACES:
                        step(ATT_PLACES[j], tp, tg)

            pe.wait_ge(const_ready, 2)
            pe.wait_ge(w_ready, 1)
            pe.wait_ge(ones_ready, 2)
            for s in ["T0", "W0T1", "W1"]:
                step(s, PRE, 0)
            for p in range(6):
                if p == ATT:
                    for k in range(LEAD):
                        cosines(0, 0, k, k)
                    att_group(0, 1, NG - 1)
                    with pe.Fori(1, NG - 1) as g:
                        att_group(g, ATT, g - 1)
                    att_group(NG - 1, ATT, NG - 2, last_group=True)
                else:
                    group(p, 0, p - 1, NG - 1)
                    with pe.Fori(1, NG) as g:
                        group(p, g, p, g - 1)

        @block.scalar
        def _(act):
            for q in range(NG):
                if q == 1:
                    for src, dst in zip([w0, wg, w2, w3a, w3b], wraw):
                        act.dma_start(dst, src).then_inc(w_loaded, 16)
                act.dma_start(xres[:, GB * q:GB * (q + 1), :].rearrange("p b n -> p (b n)"),
                              x[q * P:(q + 1) * P, :]).then_inc(x_loaded[q], 16)
            with nc.allow_non_contiguous_dma(reason="the diagonal's elements lie apart"):
                row = GB * GR
                for r in range(GB):
                    src = bass.AP(adj_t.tensor, r * (GR + P), [[row + 1, P], [(NC + 1) * P * row, NG]])
                    act.dma_start(diag[:, :].rearrange("p (q r) -> p q r", r=GB)[:, :, r], src)\
                        .then_inc(diag_loaded, 16)
            act.dma_start(bg[:, :], bias_g[0:1, :].to_broadcast([P, F])).then_inc(b_loaded, 16)
            act.dma_start(b2[:, :], bias_2[0:1, :].to_broadcast([P, F])).then_inc(b_loaded, 16)
            act.wait_ge(w_loaded, 16 * 5)
            nc.scalar.activation(wsp[:, 0, :], shared[:, 0:wofs[5]], ACT.Copy, scale=W_SCALE).then_inc(w_hi, 1)

            def split(p, g, c):
                act.wait_ge(adj_loaded[c % 2], (all_chunk_no(p, g, 0) // 2 + c // 2 + 1) * 16
                            if isinstance(g, int) else (g + NG * p) * (16 * NC // 2) + (c // 2 + 1) * 16)
                first = isinstance(g, int) and g == 0
                if c >= 2:
                    act.wait_ge(chunk_done, at(PLAIN, p, g, NC - 1, c - 1))
                elif not (first and p == 0):
                    if c == 1:
                        act.wait_ge(acc_ready, at(ALL, p, g, GB, 0))
                    elif first and p == ATT + 1:
                        act.wait_ge(block_done, (NB - 1) * (NG - 1) + NB - GB)
                    else:
                        act.wait_ge(chunk_done, at(PLAIN, p, g, NC - 1, 0))
                nc.scalar.activation(ahi[:, c % 2, :, :], adj[:, c % 2, :, :], ACT.Copy, scale=ADJ_SCALE)\
                    .then_inc(split_hi, 1)

            def ev_used(p, g):
                if p in SELF:
                    act.wait_ge(sum_hi, at(SELF, p, g))
                    if p == 0:
                        act.wait_ge(row_ready, at([0], p, g, 2, 2))
                elif p in SCALED:
                    act.wait_ge(scaled, at(SCALED, p, g, GB, GB))
                else:
                    act.wait_ge(preact, at([4, 5], p, g))

            def evacuate(p, g):
                if not isinstance(g, int) or g > 0:
                    ev_used(p, g - 1)
                elif p > 0:
                    ev_used(p - 1, NG - 1)
                n = F + 1 if p in (0, ATT) else F
                for b in range(GB):
                    act.wait_ge(acc_ready, at(ALL, p, g, GB, b + 1))
                    nc.scalar.activation(ev[:, b, 0:n], acc[:, b, 0:n], ACT.Copy,
                                         scale=1.0 if p == ATT else 1.0 / ADJ_SCALE).then_inc(ev_ready, 1)

            def blocks(g, b, n=1):
                return bass.ds(g * GB + b, n)

            def hi_of_t(p, g):
                act.wait_ge(sum_ready, at(SELF, p, g))
                for b in range(GB):
                    nc.scalar.activation(mov[1][:, blocks(g, b), 0:F], o[:, b, :], ACT.Copy, scale=d[:, blocks(g, b)])\
                        .then_inc(mov_hi, 1)

            def hi_of_h(p, g):
                if p == 4:
                    act.wait_ge(preact, at([4, 5], p, g))
                else:
                    act.wait_ge(normed, at(NORM, p, g, GB, GB))
                if not isinstance(g, int) or g > 0:
                    act.wait_ge(h_turned, at(SMALL, p, g - 1, 2, 2))
                    if p == 1:
                        act.wait_ge(gn_turned, at([1], p, g - 1, 2, 2))
                elif p > PRE:
                    act.wait_ge(h_turned, at(SMALL, SMALL[SMALL.index(p) - 1], NG - 1, 2, 2))
                    if p == 2:
                        act.wait_ge(gn_turned, at([1], 1, NG - 1, 2, 2))
                nc.scalar.activation(hsp[:, 0, :, :], o[:, :, :], ACT.Relu).then_inc(h_hi, 1)

            def keep_hT(p, g, r):
                act.wait_ge(h_turned, at(SMALL, p, g, 2, r + 1))
                if not isinstance(g, int) or g > 0:
                    act.wait_ge(small_ready, at(SMALL, p, g - 1, 2, r + 1))
                elif p > PRE:
                    act.wait_ge(small_ready, at(SMALL, SMALL[SMALL.index(p) - 1], NG - 1, 2, r + 1))
                nc.scalar.activation(hT[:, :, 2 * P * r:2 * P * (r + 1)], psT[:, :, :], ACT.Copy)\
                    .then_inc(hT_ready, 1)

            def small_out(p, b):
                if SMALL_N[p] == F:
                    return psW[:, (b % 2) * F:(b % 2 + 1) * F]
                return psW[:, F:2 * F] if b % 2 == 0 else psS[:, 0, F:2 * F]

            def hi_of_small(p, g, r):
                act.wait_ge(small_ready, at(SMALL, p, g, 2, r + 1))
                for b in (2 * r, 2 * r + 1):
                    if p in DIRECT:
                        src = psW[:, 0:F] if b % 2 == 0 else psS[:, 0, 0:F]
                        nc.scalar.activation(direct[:, blocks(g, b), :], src, ACT.Copy, scale=1.0 / W_SCALE)\
                            .then_inc(direct_ready, 1)
                    if p == 1:
                        nc.scalar.activation(junk[:, b, :], small_out(p, b), ACT.Square, scale=1.0 / W_SCALE,
                                             accum_out=ssq[:, b:b + 1]).then_inc(ssq_ready, 1)
                    nc.scalar.activation(mov[(p + 1) % 2][:, blocks(g, b), 0:F], small_out(p, b), ACT.Copy,
                                         scale=dinv_w[:, blocks(g, b)] if p == 2 else 1.0 / W_SCALE)\
                        .then_inc(mov_hi, 1)

            def hi_of_gn(p, g, r):
                act.wait_ge(rnorm_ready, at([1], p, g, 2, r + 1))
                act.wait_ge(mov_ready, at(MOVE, p, g, GB, 2 * r + 2))
                act.wait_ge(h_turned, at(SMALL, p, g, 2, r + 1))
                for b in (2 * r, 2 * r + 1):
                    nc.scalar.activation(hsp[:, 0, b, :], small_out(p, b), ACT.Copy, scale=rnorm[:, b:b + 1])\
                        .then_inc(gn_hi, 1)

            def keep_gnT(p, g, r):
                act.wait_ge(gn_turned, at([1], p, g, 2, r + 1))
                nc.scalar.activation(gnT[:, :, bass.ds(g * GR + 2 * P * r, 2 * P)], psT[:, :, :], ACT.Copy)\
                    .then_inc(gnT_ready, 1)

            def stage(name, p, g):
                if name == "ev":
                    evacuate(p, g)
                elif name == "h":
                    if p == 0:
                        hi_of_t(p, g)
                    elif p in SMALL:
                        hi_of_h(p, g)
                elif p in SMALL and name == "T0":
                    keep_hT(p, g, 0)
                elif p in SMALL and name == "W0":
                    hi_of_small(p, g, 0)
                elif p in SMALL and name == "T1":
                    keep_hT(p, g, 1)
                elif p in SMALL and name == "W1":
                    hi_of_small(p, g, 1)
                elif p == 1 and name in ("n0", "n1"):
                    hi_of_gn(p, g, int(name[1]))
                elif p == 1 and name in ("g0", "g1"):
                    keep_gnT(p, g, int(name[1]))

            PLACES = {0: ["ev"], 3: ["h"], 4: ["T0"], 5: ["W0", "T1", "n0"], 6: ["W1", "n1"], 7: ["g0", "g1"]}
            ATT_PLACES = {2: ["ev"], 10: ["h"], 12: ["T0"], 14: ["W0", "T1"], 15: ["n0"], 17: ["W1"],
                          18: ["n1"], 20: ["g0"], 22: ["g1"]}

            def group(p, g, tp, tg):
                for c in range(NC):
                    split(p, g, c)
                    for name in PLACES.get(c, []):
                        stage(name, tp, tg)

            def exponential(g, j):
                act.wait_ge(sim_ready, g * NB + j + 1)
                if not (isinstance(g, int) and g == 0 and j < GB):
                    act.wait_ge(num_split, g * NB + j + 1 - GB)
                nc.scalar.activation(expo[:, j % GB, :], psS[:, j % 2, :], ACT.Exp,
                                     scale=1.0 / (GN_SCALE * GN_SCALE)).then_inc(exp_ready, 1)

            def hi_of_numerators(g, j):
                act.wait_ge(num_ready, g * NB + j + 1)
                if isinstance(g, int) and g == 0 and j < 2 * GB:
                    if j == 0:
                        act.wait_ge(chunk_done, 2 * NG * (NC - 1))
                    elif j == GB:
                        act.wait_ge(acc_ready, 2 * NG * GB)
                elif j >= 2 * GB:
                    act.wait_ge(block_done, g * (NB - 1) + j + 1 - 2 * GB)
                elif j == 2 * GB - 1:
                    act.wait_ge(acc_ready, at(ALL, ATT, g, GB, 0))
                else:
                    act.wait_ge(block_done, (g - 1) * (NB - 1) + NB + j + 1 - 2 * GB)
                nc.scalar.activation(ahi[:, (j // GB) % 2, j % GB, :], expo[:, j % GB, :], ACT.Copy, scale=P_SCALE)\
                    .then_inc(num_hi, 1)

            def att_group(g, tp, tg):
                for j in range(NB):
                    exponential(g, j)
                    if not (isinstance(g, int) and g == 0 and j == 0):
                        hi_of_numerators(g, j - 1)
                    for name in ATT_PLACES.get(j, []):
                        stage(name, tp, tg)

            names = ["h", "T0", "W0", "T1", "W1"]
            for name in names:
                stage(name, PRE, 0)
            split(0, 0, 0)
            split(0, 0, 1)
            for q in range(1, NG):
                for name in names:
                    stage(name, PRE, q)
                if q + 1 < NC:
                    split(0, 0, q + 1)
            act.wait_ge(d_ready, 1)
            for p in range(6):
                if p == ATT:
                    act.wait_ge(dinv_ready, 2 * NG)
                    att_group(0, 1, NG - 1)
                    with act.Fori(1, NG) as g:
                        att_group(g, ATT, g - 1)
                    hi_of_numerators(NG - 1, NB - 1)
                else:
                    if p > 0:
                        group(p, 0, p - 1, NG - 1)
                    with act.Fori(1, NG) as g:
                        group(p, g, p, g - 1)
            stage("ev", 5, NG - 1)

        @block.vector
        def _(dve):
            for i in range(2):
                nc.vector.memset(mov[i][:, :, F:LO], 1.0).then_inc(ones_ready, 1)

            def blocks(g, b, n=1):
                return bass.ds(g * GB + b, n)

            def split(p, g, c):
                dve.wait_ge(split_hi, chunk_no(p, g, c) + 1)
                nc.vector.scalar_tensor_tensor(alo[:, c % 2, :, :].rearrange("p b n -> p (b n)"),
                                               adj[:, c % 2, :, :].rearrange("p b n -> p (b n)"), ADJ_SCALE,
                                               ahi[:, c % 2, :, :].rearrange("p b n -> p (b n)"),
                                               ALU.mult, ALU.subtract).then_inc(split_ready, 1)

            def epilogue(p, g):
                dve.wait_ge(ev_ready, at(ALL, p, g, GB, GB))
                rows = xres[:, blocks(g, 0, GB), :]
                if p in SELF:
                    own = mov[p % 2]
                    nc.vector.tensor_tensor(o[:, :, :], ev[:, :, 0:F], own[:, blocks(g, 0, GB), 0:F], ALU.add)\
                        .then_inc(sum_hi, 1)
                    if p == 0:
                        nc.vector.tensor_scalar(rowm[:, :], ev[:, :, F], 0.0, None, ALU.is_gt)\
                            .then_inc(row_ready, 1)
                        nc.vector.tensor_scalar(rowc[:, :], ev[:, :, F], TINY, None, ALU.max).then_inc(row_ready, 1)
                    dve.wait_ge(sum_hi, at(SELF, p, g))
                    nc.vector.tensor_tensor(o[:, :, :], o[:, :, :], own[:, blocks(g, 0, GB), LO:MW], ALU.add)\
                        .then_inc(sum_ready, 1)
                    dve.wait_ge(sum_ready, at(SELF, p, g))
                if p == 0:
                    return
                if p == 1:
                    for b in range(GB):
                        nc.vector.tensor_scalar(o[:, b, :], o[:, b, :], d[:, blocks(g, b)], None, ALU.mult)\
                            .then_inc(scaled, 1)
                elif p == 2:
                    nc.vector.reciprocal(rden[:, :], ev[:, :, F]).then_inc(den_ready, 1)
                    dve.wait_ge(den_ready, at([2], p, g))
                    for b in range(GB):
                        nc.vector.scalar_tensor_tensor(o[:, b, :], ev[:, b, 0:F], rden[:, b:b + 1], bg[:, :],
                                                       ALU.mult, ALU.add).then_inc(scaled, 1)
                elif p == 3:
                    for b in range(GB):
                        nc.vector.scalar_tensor_tensor(o[:, b, :], ev[:, b, 0:F], dinv[:, blocks(g, b)], b2[:, :],
                                                       ALU.mult, ALU.add).then_inc(scaled, 1)
                else:
                    dve.wait_ge(direct_ready, at(DIRECT, p - 1, g, GB, GB))
                    nc.vector.tensor_tensor(o[:, :, :], ev[:, :, 0:F], direct[:, blocks(g, 0, GB), :], ALU.add)\
                        .then_inc(preact, 1)
                if p in SCALED:
                    dve.wait_ge(scaled, at(SCALED, p, g, GB, GB))
                else:
                    dve.wait_ge(preact, at([4, 5], p, g))
                if p == 2:
                    nc.vector.tensor_tensor(rows, o[:, :, :], rows, ALU.add).then_inc(x_ready, 1)
                elif p in RES:
                    nc.vector.scalar_tensor_tensor(rows, o[:, :, :], 0.0, rows, ALU.max, ALU.add).then_inc(x_ready, 1)

            def norm_stats(p, g):
                if p == PRE:
                    dve.wait_ge(x_loaded[g], 16)
                else:
                    dve.wait_ge(x_ready, at(RES, p, g))
                dve.sem_inc(passed, 1)
                for b in range(GB):
                    nc.vector.bn_stats(stats[:, b, :], xres[:, blocks(g, b), :].rearrange("p a n -> p (a n)"))\
                        .then_inc(stats_ready, 1)
                dve.wait_ge(stats_ready, at(NORM, p, g, GB, GB))
                dve.sem_inc(passed, 1)
                for b in range(GB):
                    nc.vector.bn_aggr(mv[:, b, :], stats[:, b, :]).then_inc(mv_ready, 1)
                dve.wait_ge(mv_ready, at(NORM, p, g, GB, GB))
                nc.vector.tensor_scalar(vare[:, :], mv[:, :, 1], LN_EPS, None, ALU.add).then_inc(var_ready, 1)

            def lo_of_h(p, g):
                if p in NORM:
                    dve.wait_ge(rstd_ready, at(NORM, p, g))
                    for b in range(GB):
                        nc.vector.tensor_scalar(o[:, b, :], xres[:, blocks(g, b), :].rearrange("p a n -> p (a n)"),
                                                mv[:, b, 0:1], rstd[:, b:b + 1], ALU.subtract, ALU.mult)\
                            .then_inc(normed, 1)
                    dve.wait_ge(normed, at(NORM, p, g, GB, GB))
                dve.wait_ge(h_hi, at(SMALL, p, g))
                nc.vector.scalar_tensor_tensor(hsp[:, 1, :, :], o[:, :, :], 0.0, hsp[:, 0, :, :],
                                               ALU.max, ALU.subtract).then_inc(h_ready, 1)

            def lo_of_t(p, g):
                for b in range(GB):
                    dve.wait_ge(mov_hi, at(MOVE, p, g, GB, b + 1))
                    nc.vector.scalar_tensor_tensor(mov[1][:, blocks(g, b), LO:MW], o[:, b, :], d[:, blocks(g, b)],
                                                   mov[1][:, blocks(g, b), 0:F], ALU.mult, ALU.subtract)\
                        .then_inc(mov_ready, 1)
                dve.wait_ge(rowp_ready, at([0], p, g))
                nc.vector.tensor_tensor(dinv[:, blocks(g, 0, GB)], rowp[:, :], rowm[:, :], ALU.mult)\
                    .then_inc(dinv_ready, 1)
                nc.vector.scalar_tensor_tensor(dinv_w[:, blocks(g, 0, GB)], rowp[:, :], 1.0 / W_SCALE, rowm[:, :],
                                               ALU.mult, ALU.mult).then_inc(dinv_ready, 1)

            def small_out(p, b):
                if SMALL_N[p] == F:
                    return psW[:, (b % 2) * F:(b % 2 + 1) * F]
                return psW[:, F:2 * F] if b % 2 == 0 else psS[:, 0, F:2 * F]

            def lo_of_small(p, g, r):
                for b in (2 * r, 2 * r + 1):
                    dve.wait_ge(mov_hi, at(MOVE, p, g, GB, b + 1 if p in DIRECT else 2 * r + 2))
                    m = mov[(p + 1) % 2]
                    nc.vector.scalar_tensor_tensor(m[:, blocks(g, b), LO:MW], small_out(p, b),
                                                   dinv_w[:, blocks(g, b)] if p == 2 else 1.0 / W_SCALE,
                                                   m[:, blocks(g, b), 0:F], ALU.mult, ALU.subtract)\
                        .then_inc(mov_ready, 1)

            def guard_norm(p, g, r):
                dve.wait_ge(ssq_ready, at([1], p, g, GB, 2 * r + 2))
                nc.vector.tensor_scalar(ssqc[:, 2 * r:2 * r + 2], ssq[:, 2 * r:2 * r + 2], NORM_EPS * NORM_EPS, None,
                                        ALU.max).then_inc(ssqc_ready, 1)

            def lo_of_gn(p, g, r):
                for b in (2 * r, 2 * r + 1):
                    dve.wait_ge(gn_hi, at([1], p, g, GB, 2 * r + 2))
                    nc.vector.scalar_tensor_tensor(hsp[:, 1, b, :], small_out(p, b), rnorm[:, b:b + 1],
                                                   hsp[:, 0, b, :], ALU.mult, ALU.subtract).then_inc(gn_ready, 1)

            def stage(name, p, g):
                if name == "epi" and p >= 0:
                    epilogue(p, g)
                elif name == "stats" and p in NORM:
                    norm_stats(p, g)
                elif name == "h":
                    if p == 0:
                        lo_of_t(p, g)
                    elif p in SMALL:
                        lo_of_h(p, g)
                elif p in SMALL and name == "W0":
                    if p == 1:
                        guard_norm(p, g, 0)
                    lo_of_small(p, g, 0)
                elif p in SMALL and name == "W1":
                    if p == 1:
                        guard_norm(p, g, 1)
                    lo_of_small(p, g, 1)
                elif p == 1 and name in ("n0", "n1"):
                    lo_of_gn(p, g, int(name[1]))

            PLACES = {1: ["epi"], 2: ["stats"], 3: ["h"], 5: ["W0", "n0"], 6: ["W1", "n1"]}
            ATT_PLACES = {4: ["epi"], 7: ["stats"], 10: ["h"], 14: ["W0"], 15: ["n0"], 17: ["W1"], 18: ["n1"]}

            def group(p, g, tp, tg):
                for c in range(NC):
                    split(p, g, c)
                    for name in PLACES.get(c, []):
                        stage(name, tp, tg)

            def numerators(g, j):
                c = j // GB
                if j % GB == 0:
                    dve.wait_ge(adj_loaded[c % 2], (ATT * NG + g) * (16 * NC // 2) + (c // 2 + 1) * 16)
                dve.wait_ge(exp_ready, g * NB + j + 1)
                nc.vector.scalar_tensor_tensor(expo[:, j % GB, :], adj[:, c % 2, j % GB, :], ADJ_EPS,
                                               expo[:, j % GB, :], ALU.add, ALU.mult).then_inc(num_ready, 1)

            def lo_of_numerators(g, j):
                dve.wait_ge(num_hi, g * NB + j + 1)
                nc.vector.scalar_tensor_tensor(alo[:, (j // GB) % 2, j % GB, :], expo[:, j % GB, :], P_SCALE,
                                               ahi[:, (j // GB) % 2, j % GB, :], ALU.mult, ALU.subtract)\
                    .then_inc(num_split, 1)

            def att_group(g, tp, tg):
                for j in range(NB):
                    numerators(g, j)
                    if not (isinstance(g, int) and g == 0 and j == 0):
                        lo_of_numerators(g, j - 1)
                    for name in ATT_PLACES.get(j, []):
                        stage(name, tp, tg)

            stage("stats", PRE, 0)
            dve.wait_ge(diag_loaded, 16 * GB)
            nc.vector.tensor_scalar(diag[:, :], diag[:, :], 1.0, None, ALU.add).then_inc(diag_one, 1)
            stage("h", PRE, 0)
            dve.wait_ge(w_hi, 1)
            nc.vector.scalar_tensor_tensor(wsp[:, 1, :], shared[:, 0:wofs[5]], W_SCALE, wsp[:, 0, :],
                                           ALU.mult, ALU.subtract).then_inc(w_ready, 1)
            stage("W0", PRE, 0)
            stage("W1", PRE, 0)
            split(0, 0, 0)
            split(0, 0, 1)
            for q in range(1, NG):
                for name in ["stats", "h", "W0", "W1"]:
                    stage(name, PRE, q)
                if q + 1 < NC:
                    split(0, 0, q + 1)
            dve.wait_ge(d_ready, 1)
            dve.wait_ge(b_loaded, 32)
            for p in range(6):
                if p == ATT:
                    dve.wait_ge(dinv_ready, 2 * NG)
                    att_group(0, 1, NG - 1)
                    with dve.Fori(1, NG) as g:
                        att_group(g, ATT, g - 1)
                    lo_of_numerators(NG - 1, NB - 1)
                else:
                    if p > 0:
                        group(p, 0, p - 1, NG - 1)
                    with dve.Fori(1, NG) as g:
                        group(p, g, p, g - 1)
            epilogue(5, NG - 1)


def kernel(x, adj, L0_gnn_W, L1_gnn_weight, L1_gnn_bias, L2_gnn_W, L2_gnn_b, L3_gnn_W1, L3_gnn_W2):
    import concourse.bacc as bacc
    from concourse.bass_utils import run_bass_kernel_spmd

    def rows_on_partitions(w):
        return w.reshape(-1, P, w.shape[1]).transpose(1, 0, 2)

    def halves(w):
        return rows_on_partitions(np.concatenate([w[:F], w[F:]], axis=1))

    arrays = {
        "x": np.asarray(x).reshape(NG, GB, P, F).transpose(0, 2, 1, 3).reshape(NG * P, GB * F),
        "adj_t": np.asarray(adj).reshape(NG, GR, NC, GB, P).transpose(0, 2, 4, 3, 1).reshape(NG * NC * P, GB * GR),
        "w0": rows_on_partitions(np.asarray(L0_gnn_W).T),
        "wg": rows_on_partitions(np.asarray(L1_gnn_weight)),
        "bias_g": np.asarray(L1_gnn_bias).reshape(1, F),
        "w2": rows_on_partitions(np.asarray(L2_gnn_W)),
        "bias_2": np.asarray(L2_gnn_b).reshape(1, F),
        "w3a": halves(np.asarray(L3_gnn_W1)),
        "w3b": halves(np.asarray(L3_gnn_W2)),
    }
    nc = bacc.Bacc("TRN2", target_bir_lowering=False, num_devices=1)
    aps = {}
    for name, a in arrays.items():
        arrays[name] = np.ascontiguousarray(a)
        aps[name] = nc.dram_tensor(f"in_{name}", a.shape, mybir.dt.from_np(a.dtype), kind="ExternalInput").ap()
    out = nc.dram_tensor("out", (N, F), mybir.dt.float32, kind="ExternalOutput").ap()
    build(nc, out=out, **aps)
    r = run_bass_kernel_spmd(nc, [{f"in_{name}": a for name, a in arrays.items()}], core_ids=[0])
    return r.results[0]["out"]
```

```python
from contextlib import ExitStack

import concourse.bass as bass
import numpy as np
from concourse import mybir

N = 4096
F = 256
P = 128
NB = N // P
GB = 4
NG = NB // GB
NC = NB // GB
GR = GB * P
FB = F // P
MW = 2 * F + 2
LO = F + 2
LN_EPS = 1e-5
ADJ_EPS = 1e-8
NORM_EPS = 1e-8
TINY = 1.2e-38
ADJ_SCALE = 256.0
W_SCALE = 64.0
P_SCALE = 4096.0
GN_SCALE = 64.0
LEAD = 3
HALF = GB // 2
NH = NB // HALF
NUMS = 3
PRE = -1
ATT = 2

SMALL_N = {PRE: F, 1: F, 2: F, 3: 2 * F, 4: 2 * F}


def build(nc, x, adj_t, w0, wg, bias_g, w2, bias_2, w3a, w3b, sent, out):
    f32, f16 = mybir.dt.float32, mybir.dt.float16
    ALU, ACT = mybir.AluOpType, mybir.ActivationFunctionType

    ctx = ExitStack()
    with ctx:
        def sb(name, shape, dt):
            return ctx.enter_context(nc.sbuf_tensor(name, shape, dt))

        def pb(name, shape, dt):
            return ctx.enter_context(nc.psum_tensor(name, shape, dt))

        def sem(name):
            return ctx.enter_context(nc.semaphore(name))

        xres = sb("xres", [P, NB, F], f32)
        mov = [sb(f"mov{i}", [P, NB, MW], f16) for i in range(2)]
        shared = sb("shared", [P, 2 * FB * N // 2], f32)
        gnT = shared[:, :].bitcast(f16).rearrange("p (q n) -> p q n", q=2 * FB)
        direct = shared[:, :].rearrange("p (b n) -> p b n", n=F)
        wcols = [F, F, F, 2 * F, 2 * F]
        wofs = [sum(wcols[:i]) * FB for i in range(6)]
        wraw = [shared[:, wofs[i]:wofs[i + 1]].rearrange("p (f n) -> p f n", f=FB) for i in range(5)]
        wsp = sb("wsp", [P, 2, wofs[5]], f16)
        wpart = [[wsp[:, s, wofs[i]:wofs[i + 1]].rearrange("p (f n) -> p f n", f=FB) for s in range(2)]
                 for i in range(5)]
        weights_of = {PRE: wpart[0], 1: wpart[1], 2: wpart[2], 3: wpart[3], 4: wpart[4]}
        adj = sb("adj", [P, 2, GB, GR], f32)
        ahi = sb("ahi", [P, 2, GB, GR], f16)
        alo = sb("alo", [P, 2, GB, GR], f16)
        expo = sb("expo", [P, 4, HALF * GR], f32)
        nums = sb("nums", [P, NUMS, GR], f32)
        ev = sb("ev", [P, GB, F + 1], f32)
        o = sb("o", [P, GB, F], f32)
        hsp = sb("hsp", [P, 2, GB, F], f16)
        o2 = expo[:, 0, :].rearrange("p (b n) -> p b n", b=GB)
        hsp2 = expo[:, 1, :].bitcast(f16).rearrange("p (s b n) -> p s b n", s=2, b=GB)
        own = sb("own", [P, GB, F], f32)
        hT = sb("hT", [P, 2 * FB, GR], f16)
        bg = sb("bg", [P, F], f32)
        b2 = sb("b2", [P, F], f32)
        ident = sb("ident", [P, P], f16)
        ident32 = sb("ident32", [P, P], f32)
        diag = sb("diag", [P, NB], f32)
        d = sb("d", [P, NB], f32)
        dinv = sb("dinv", [P, NB], f32)
        dinv_w = sb("dinv_w", [P, NB], f32)
        neghalf = sb("neghalf", [P, NB], f32)
        stats = sb("stats", [P, GB, 6], f32)
        mv = sb("mv", [P, 2, GB, 2], f32)
        vare = sb("vare", [P, 2, GB], f32)
        rstd = sb("rstd", [P, 2, GB], f32)
        nmean = sb("nmean", [P, 2, GB], f32)
        shift = sb("shift", [P, 2, GB], f32)
        rowc = sb("rowc", [P, GB], f32)
        rowm = sb("rowm", [P, GB], f32)
        rowp = sb("rowp", [P, GB], f32)
        rden = sb("rden", [P, GB], f32)
        ssq = sb("ssq", [P, GB], f32)
        ssqc = sb("ssqc", [P, GB], f32)
        rnorm = sb("rnorm", [P, GB], f32)
        junk = sb("junk", [P, GB, F], f16)

        acc = pb("acc", [P, GB, GR], f32)
        psT = pb("psT", [P, 2 * FB, 2 * P], f16)
        psW = pb("psW", [P, 2 * F], f32)
        psS = pb("psS", [P, 2, GR], f32)
        psT2 = psS[:, 0, :].bitcast(f16).rearrange("p (q n) -> p q n", q=2 * FB)

        w0_loaded = sem("w0_loaded")
        w_loaded = sem("w_loaded")
        b_loaded = sem("b_loaded")
        diag_loaded = sem("diag_loaded")
        x_loaded = [sem(f"x_loaded{q}") for q in range(NG)]
        adj_loaded = [sem(f"adj_loaded{s}") for s in range(2)]
        half_loaded = [sem(f"half_loaded{q}") for q in range(4)]
        exp_sent = [sem(f"exp_sent{q}") for q in range(4)]
        exp_back = [sem(f"exp_back{q}") for q in range(4)]
        stored = sem("stored")
        const_ready = sem("const_ready")
        ident_zero = sem("ident_zero")
        ones_ready = sem("ones_ready")
        w_hi = sem("w_hi")
        w_ready = sem("w_ready")
        diag_one = sem("diag_one")
        d_ready = sem("d_ready")
        split_hi = sem("split_hi")
        split_ready = sem("split_ready")
        chunk_done = sem("chunk_done")
        exp_ready = sem("exp_ready")
        sim_ready = sem("sim_ready")
        num_ready = sem("num_ready")
        num_hi = sem("num_hi")
        num_split = sem("num_split")
        block_done = sem("block_done")
        acc_ready = sem("acc_ready")
        ev_ready = sem("ev_ready")
        own_ready = sem("own_ready")
        sum_ready = sem("sum_ready")
        row_ready = sem("row_ready")
        rowp_ready = sem("rowp_ready")
        dinv_ready = sem("dinv_ready")
        den_ready = sem("den_ready")
        scaled = sem("scaled")
        preact = sem("preact")
        x_ready = sem("x_ready")
        stats_ready = sem("stats_ready")
        passed = sem("passed")
        mv_ready = sem("mv_ready")
        var_ready = sem("var_ready")
        rstd_ready = sem("rstd_ready")
        shift_ready = sem("shift_ready")
        normed = sem("normed")
        h_hi = sem("h_hi")
        h_ready = sem("h_ready")
        h_turned = sem("h_turned")
        hT_ready = sem("hT_ready")
        small_ready = sem("small_ready")
        direct_ready = sem("direct_ready")
        mov_hi = sem("mov_hi")
        mov_ready = sem("mov_ready")
        ssq_ready = sem("ssq_ready")
        ssqc_ready = sem("ssqc_ready")
        rnorm_ready = sem("rnorm_ready")
        gn_hi = sem("gn_hi")
        gn_ready = sem("gn_ready")
        gn_turned = sem("gn_turned")
        gnT_ready = sem("gnT_ready")

        ALL = [0, 1, 2, 3, 4, 5]
        NORM = [PRE, 1, 2, 3]
        SMALL = [PRE, 1, 2, 3, 4]
        SELF = [0, 1]
        RES = [1, 2, 3, 5]
        SCALED = [1, 2, 3]
        DIRECT = [3, 4]
        MOVE = [PRE, 0, 1, 2, 3, 4]

        def at(passes, p, g, per=1, k=1):
            return (g + NG * passes.index(p)) * per + k

        PLAIN = [0, 1, 3, 4, 5]

        def chunk_no(p, g, c):
            return (g + NG * PLAIN.index(p)) * NC + c

        def computed(g, j):
            return j >= GB * g

        def is_sent(g, H):
            return H >= NH // NC * (g + 1)

        def exp_no(g, j):
            return sum(NB - GB * h for h in range(g)) + j - GB * g + 1

        def sent_no(g, H):
            return sum(is_sent(a, b) and b % 4 == H % 4 and (a, b) <= (g, H) for a in range(NG) for b in range(NH))

        def back_no(g, H):
            return sum(not computed(a, HALF * b) and b % 4 == H % 4 and (a, b) <= (g, H)
                       for a in range(NG) for b in range(NH))

        def exp_slot_free(eng, g, H):
            g, H = (g, H - 4) if H >= 4 else (g - 1, H - 4 + NH)
            if g < 0:
                return
            if computed(g, HALF * H):
                eng.wait_ge(num_ready, g * NB + HALF * (H + 1))
                if is_sent(g, H):
                    eng.wait_ge(exp_sent[H % 4], 32 * sent_no(g, H))
            else:
                eng.wait_ge(sim_ready, g * NB + HALF * (H + 1))

        def sent_rows(g, c):
            return 2 * P * (sum(NC - 1 - h for h in range(g)) + c - g - 1)

        def work(p, g):
            return (o2, hsp2, 1) if p == PRE and g % 2 else (o, hsp, 0)

        def small_bank(p, b):
            if SMALL_N[p] == 2 * F:
                return psW[:, :] if b % 2 == 0 else psS[:, 0, :]
            bank = psS[:, 1, :] if p == PRE and b >= 2 else psW
            return bank[:, (b % 2) * F:(b % 2 + 1) * F]

        block = ctx.enter_context(nc.Block())

        @block.sync
        def _(sp):
            def load_x(q):
                sp.dma_start(xres[:, GB * q:GB * (q + 1), :].rearrange("p b n -> p (b n)"),
                             x[q * P:(q + 1) * P, :]).then_inc(x_loaded[q], 16)

            def load(p, g, c, first=False):
                if not first:
                    q, h, e = (p, g, c - 2) if c >= 2 else ((p, g - 1, c + 6) if not isinstance(g, int) or g > 0
                                                            else (p - 1, NG - 1, c + 6))
                    if q == ATT:
                        sp.wait_ge(num_ready, h * NB + GB * (e + 1))
                    else:
                        sp.wait_ge(split_ready, chunk_no(q, h, e) + 1)
                row = g * (NC * P) + c * P
                sp.dma_start(adj[:, c % 2, :, :].rearrange("p b n -> p (b n)"), adj_t[bass.ds(row, P), :])\
                    .then_inc(adj_loaded[c % 2], 16)

            def store(g):
                sp.wait_ge(x_ready, at(RES, 5, g))
                sp.dma_start(out[bass.ds(g * GR, GR), :].rearrange("(b p) n -> p b n", p=P),
                             xres[:, bass.ds(g * GB, GB), :]).then_inc(stored, 16)

            def group(p, g, first=False):
                for c in range(NC):
                    load(p, g, c, first and c < 2)
                    if p == 5 and c == 5 and not isinstance(g, int):
                        store(g - 1)

            def send(g, H):
                sp.wait_ge(exp_ready, exp_no(g, HALF * H + HALF - 1))
                k = H % 2 * HALF
                rows = sent_rows(g, H // 2)
                to = sent[rows:rows + 2 * P, k * GR // 2:(k + HALF) * GR // 2]
                for e in range(2):
                    sp.dma_start(to[e * P:(e + 1) * P, :].rearrange("p (b n) -> p b n", b=HALF),
                                 expo[:, H % 4, :].rearrange("p (b n) -> p b n", b=HALF)[:, :, e * GR // 2:(e + 1) * GR // 2])\
                        .then_inc(exp_sent[H % 4], 16)

            def att_half(g, H):
                c = H // 2
                if g == 0 and H < 4:
                    sp.wait_ge(split_ready, chunk_no(ATT - 1, NG - 1, NC - 2 + c) + 1)
                else:
                    sp.wait_ge(num_ready, g * NB + HALF * (H - 3))
                row = (g * NC + c) * P
                cols = slice(H % 2 * HALF * GR, (H % 2 + 1) * HALF * GR)
                sp.dma_start(adj[:, c % 2, H % 2 * HALF:(H % 2 + 1) * HALF, :].rearrange("p b n -> p (b n)"),
                             adj_t[row:row + P, cols]).then_inc(half_loaded[H % 4], 16)
                if not computed(g, HALF * H):
                    exp_slot_free(sp, g, H)
                    for a in range(2):
                        sp.wait_ge(exp_sent[(2 * g + a) % 4], 32 * sent_no(c, 2 * g + a))
                    rows = sent_rows(c, g) + H % 2 * P
                    sp.dma_start(expo[:, H % 4, :], sent[rows:rows + P, :]).then_inc(exp_back[H % 4], 16)

            sp.wait_ge(x_loaded[0], 16)
            for q in range(1, NG):
                load_x(q)
            for p in range(6):
                if p == ATT:
                    for g in range(NG):
                        for H in range(NH):
                            before = (g, H - 4) if H >= 4 else (g - 1, H - 4 + NH)
                            if before[0] >= 0 and is_sent(*before):
                                send(*before)
                            att_half(g, H)
                else:
                    group(p, 0, first=p == 0)
                    with sp.Fori(1, NG) as g:
                        group(p, g)
            for b in range(GB):
                sp.wait_ge(x_ready, at(RES, 5, NG - 1, 1, b + 1))
                row = (NG - 1) * GR + b * P
                sp.dma_start(out[row:row + P, :], xres[:, (NG - 1) * GB + b, :]).then_inc(stored, 16)
            sp.wait_ge(stored, 16 * (NG - 1 + GB))

        @block.gpsimd
        def _(pool):
            nc.gpsimd.memset(ident[:, :], 0.0).then_inc(ident_zero, 1)
            nc.gpsimd.memset(neghalf[:, :], -0.5).then_inc(const_ready, 1)
            nc.gpsimd.memset(ident32[:, :], 0.0).then_inc(ident_zero, 1)
            pool.wait_ge(ident_zero, 2)
            nc.gpsimd.affine_select(out=ident32[:, :], in_=ident32[:, :], compare_op=ALU.not_equal, fill=1.0,
                                    base=0, pattern=[[-1, P]], channel_multiplier=1).then_inc(const_ready, 1)
            nc.gpsimd.affine_select(out=ident[:, :], in_=ident[:, :], compare_op=ALU.not_equal, fill=1.0,
                                    base=0, pattern=[[-1, P]], channel_multiplier=1).then_inc(const_ready, 1)
            pool.wait_ge(const_ready, 3)

            def rstd_of(p, g, u=0):
                pool.wait_ge(var_ready, at(NORM, p, g, 2, 2))
                nc.gpsimd.tensor_tensor(out=rstd[:, u, :], in0=vare[:, u, :], in1=neghalf[:, 0:GB], op=ALU.pow)\
                    .then_inc(rstd_ready, 1)
                pool.wait_ge(rstd_ready, at(NORM, p, g))
                nc.gpsimd.tensor_tensor(out=shift[:, u, :], in0=nmean[:, u, :], in1=rstd[:, u, :], op=ALU.mult)\
                    .then_inc(shift_ready, 1)

            def tail(p, g):
                if p in SELF:
                    pool.wait_ge(mov_ready, at(MOVE, p - 1, g, GB, GB))
                    if not (isinstance(g, int) and p == 0):
                        pool.wait_ge(sum_ready, at(SELF, p, g, 1, 0))
                    rows = mov[p % 2][:, bass.ds(g * GB, GB), :]
                    nc.gpsimd.tensor_tensor(out=own[:, :, :], in0=rows[:, :, 0:F], in1=rows[:, :, LO:MW], op=ALU.add)\
                        .then_inc(own_ready, 1)
                if p == 0:
                    pool.wait_ge(row_ready, at([0], p, g, 2, 2))
                    nc.gpsimd.tensor_tensor(out=rowp[:, :], in0=rowc[:, :], in1=neghalf[:, 0:GB], op=ALU.pow)\
                        .then_inc(rowp_ready, 1)
                if p in NORM:
                    rstd_of(p, g)
                if p == 1:
                    for r in range(2):
                        pool.wait_ge(ssqc_ready, at([1], p, g, 2, r + 1))
                        nc.gpsimd.tensor_tensor(out=rnorm[:, 2 * r:2 * r + 2], in0=ssqc[:, 2 * r:2 * r + 2],
                                                in1=neghalf[:, 0:2], op=ALU.pow).then_inc(rnorm_ready, 1)

            with pool.Fori(0, NG, 2) as g:
                rstd_of(PRE, g, 0)
                rstd_of(PRE, g + 1, 1)
            pool.wait_ge(diag_one, 1)
            nc.gpsimd.tensor_tensor(out=d[:, :], in0=diag[:, :], in1=neghalf[:, :], op=ALU.pow).then_inc(d_ready, 1)
            for p in [0, 1, 2, 3]:
                if p == 0:
                    tail(0, 0)
                    with pool.Fori(1, NG) as g:
                        tail(p, g)
                else:
                    with pool.Fori(0, NG) as g:
                        tail(p, g)

        @block.tensor
        def _(pe):
            def product(p, g, c, b, k, first, last):
                jb = GB * c + k
                m = mov[p % 2]
                n = F + 1 if p in (0, ATT) else F
                cols = slice(b * P, (b + 1) * P)
                hi, lo = ahi[:, c % 2, k, cols], alo[:, c % 2, k, cols]
                nc.tensor.matmul(acc[:, b, 0:n], hi, m[:, jb, 0:n], start=first, stop=False)
                nc.tensor.matmul(acc[:, b, 0:F], hi, m[:, jb, LO:LO + F], start=False, stop=False)
                return nc.tensor.matmul(acc[:, b, 0:n], lo, m[:, jb, 0:n], start=False, stop=last)

            def bank_free(p, g, b):
                if isinstance(g, int) and g == 0:
                    if p > 0:
                        pe.wait_ge(ev_ready, at(ALL, p - 1, NG - 1, GB, b + 1))
                else:
                    pe.wait_ge(ev_ready, at(ALL, p, g - 1, GB, b + 1))

            def turn(p, g, r):
                pe.wait_ge(h_ready, at(SMALL, p, g))
                if p == PRE:
                    if g > 0:
                        pe.wait_ge(hT_ready, at(SMALL, p, g - 1, 2, r + 1))
                elif r == 1:
                    pe.wait_ge(hT_ready, at(SMALL, p, g, 2, 1))
                elif not isinstance(g, int) or g > 0:
                    pe.wait_ge(hT_ready, at(SMALL, p, g - 1, 2, 2))
                    if p == 1:
                        pe.wait_ge(gnT_ready, at([1], p, g - 1, 2, 2))
                else:
                    before = SMALL[SMALL.index(p) - 1]
                    pe.wait_ge(hT_ready, at(SMALL, before, NG - 1, 2, 2))
                    if p == 2:
                        pe.wait_ge(gnT_ready, at([1], 1, NG - 1, 2, 2))
                transposes(r, work(p, g)[1], psT2 if p == PRE and r == 1 else psT).then_inc(h_turned, 1)

            def transposes(r, hsp, to):
                for q in range(2 * FB):
                    for b in range(2):
                        last = nc.tensor.transpose(to[:, q, b * P:(b + 1) * P],
                                                   hsp[:, q // FB, 2 * r + b, (q % FB) * P:(q % FB + 1) * P],
                                                   ident[:, :])
                return last

            def small(p, g, r):
                whi, wlo = weights_of[p]
                pe.wait_ge(hT_ready, at(SMALL, p, g, 2, r + 1))
                if p == PRE:
                    if g > 0:
                        pe.wait_ge(mov_ready, at(MOVE, p, g - 1, GB, 2 * r + 2))
                elif r == 1:
                    pe.wait_ge(mov_ready, at(MOVE, p, g, GB, 2))
                    if p == 1:
                        pe.wait_ge(gn_ready, at([1], p, g, GB, 2))
                elif not isinstance(g, int) or g > 0:
                    pe.wait_ge(mov_ready, at(MOVE, p, g - 1, GB, 4))
                    if p == 1:
                        pe.wait_ge(gn_ready, at([1], p, g - 1, GB, 4))
                elif p > PRE:
                    pe.wait_ge(mov_ready, at(MOVE, p - 1, NG - 1, GB, 4))
                    if p == 2:
                        pe.wait_ge(gn_ready, at([1], 1, NG - 1, GB, 4))
                for b in range(2):
                    rows = slice((2 * r + b) * P, (2 * r + b + 1) * P)
                    to = small_bank(p, 2 * r + b)
                    for f in range(FB):
                        nc.tensor.matmul(to, hT[:, f, rows], whi[:, f, :], start=f == 0, stop=False)
                        nc.tensor.matmul(to, hT[:, f, rows], wlo[:, f, :], start=False, stop=False)
                        last = nc.tensor.matmul(to, hT[:, FB + f, rows], whi[:, f, :], start=False,
                                                stop=f == FB - 1)
                last.then_inc(small_ready, 1)

            def turn_gn(p, g, r):
                pe.wait_ge(gn_ready, at([1], p, g, GB, 2 * r + 2))
                if r == 0:
                    pe.wait_ge(hT_ready, at(SMALL, p, g, 2, 2))
                else:
                    pe.wait_ge(gnT_ready, at([1], p, g, 2, 1))
                transposes(r, hsp, psT).then_inc(gn_turned, 1)

            def step(name, p, g):
                if name == "T0":
                    turn(p, g, 0)
                elif name == "W0T1":
                    small(p, g, 0)
                    turn(p, g, 1)
                elif name == "W1":
                    small(p, g, 1)
                elif name == "T0T1":
                    turn(p, g, 0)
                    turn(p, g, 1)
                elif name == "W0":
                    small(p, g, 0)
                elif p == 1:
                    turn_gn(p, g, int(name[1]))

            PLACES = {(3, 3): "T0", (4, 0): "W0T1", (5, 0): "W1", (6, 0): "G0", (6, 2): "G1"}
            ATT_PLACES = [{10: "T0", 12: "W0T1", 15: "W1", 18: "G0", 20: "G1"}, {19: "T0", 22: "W0T1", 26: "W1"}]

            def moving_there(p, g, c):
                if isinstance(g, int) and g == 0:
                    pe.wait_ge(mov_ready, at(MOVE, p - 1, c, GB, 4))

            def group(p, g, tp, tg):
                for c in range(NC):
                    pe.wait_ge(split_ready, chunk_no(p, g, c) + 1)
                    moving_there(p, g, c)
                    for b in range(GB):
                        if c == 0:
                            bank_free(p, g, b)
                        for k in range(GB):
                            last = product(p, g, c, b, k, c == 0 and k == 0, c == NC - 1 and k == GB - 1)
                        if c == NC - 1:
                            last.then_inc(acc_ready, 1)
                        elif b == GB - 1:
                            last.then_inc(chunk_done, 1)
                        if tp in SMALL and tp != PRE and (c, b) in PLACES:
                            step(PLACES[c, b], tp, tg)
                        if tp == PRE and c + 2 < NC and b < 3:
                            step(["T0T1", "W0", "W1"][b], PRE, c + 2)

            def similarity(g, j):
                n = g * NB + j
                before = (g, j - 2) if j >= 2 else (g - 1, j - 2 + NB)
                if before[0] >= 0:
                    if computed(*before):
                        pe.wait_ge(exp_ready, exp_no(*before))
                    else:
                        pe.wait_ge(num_ready, n - 1)
                if computed(g, j):
                    cosines(g, j).then_inc(sim_ready, 1)
                    return
                H = j // HALF
                pe.wait_ge(exp_back[H % 4], 16 * back_no(g, H))
                half = expo[:, H % 4, :].rearrange("p (b n) -> p b n", b=GB)
                for b in range(GB):
                    last = nc.tensor.transpose(psS[:, j % 2, b * P:(b + 1) * P],
                                               half[:, b, (j % HALF) * P:(j % HALF + 1) * P], ident32[:, :])
                last.then_inc(sim_ready, 1)

            def cosines(g, j):
                if g == 0 and j % GB == 0:
                    pe.wait_ge(gnT_ready, at([1], 1, j // GB, 2, 2))
                rows = slice(g * GR, (g + 1) * GR)
                for f in range(FB):
                    hi, lo = gnT[:, f, j * P:(j + 1) * P], gnT[:, FB + f, j * P:(j + 1) * P]
                    mhi, mlo = gnT[:, f, rows], gnT[:, FB + f, rows]
                    nc.tensor.matmul(psS[:, j % 2, :], hi, mhi, start=f == 0, stop=False)
                    nc.tensor.matmul(psS[:, j % 2, :], hi, mlo, start=False, stop=False)
                    last = nc.tensor.matmul(psS[:, j % 2, :], lo, mhi, start=False, stop=f == FB - 1)
                return last

            def att_group(g, tp, tg):
                for j in range(NB):
                    if j + LEAD < NB:
                        similarity(g, j + LEAD)
                    elif g < NG - 1:
                        similarity(g + 1, j + LEAD - NB)
                    pe.wait_ge(num_split, g * NB + j + 1)
                    if j % GB == 0:
                        moving_there(ATT, g, j // GB)
                    for b in range(GB):
                        if j == 0:
                            bank_free(ATT, g, b)
                        last = product(ATT, g, j // GB, b, j % GB, j == 0, j == NB - 1)
                        if j == NB - 1:
                            last.then_inc(acc_ready, 1)
                        elif b == GB - 1:
                            last.then_inc(block_done, 1)
                    if j in ATT_PLACES[g > 0]:
                        step(ATT_PLACES[g > 0][j], tp, tg)

            pe.wait_ge(const_ready, 3)
            pe.wait_ge(w_ready, 1)
            pe.wait_ge(ones_ready, 2)
            for g in range(2):
                for s in ["T0T1", "W0", "W1"]:
                    step(s, PRE, g)
            for p in range(6):
                if p == 1:
                    pe.wait_ge(w_ready, 2)
                if p == ATT:
                    for j in range(LEAD):
                        similarity(0, j)
                    for g in range(NG):
                        att_group(g, *((ATT, g - 1) if g else (1, NG - 1)))
                else:
                    group(p, 0, p - 1, NG - 1)
                    with pe.Fori(1, NG) as g:
                        group(p, g, p, g - 1)

        @block.scalar
        def _(act):
            act.dma_start(xres[:, 0:GB, :].rearrange("p b n -> p (b n)"), x[0:P, :]).then_inc(x_loaded[0], 16)
            act.dma_start(wraw[0], w0).then_inc(w0_loaded, 16)

            def load_others():
                for src, dst in zip([wg, w2, w3a, w3b], wraw[1:]):
                    act.dma_start(dst, src).then_inc(w_loaded, 16)
                with nc.allow_non_contiguous_dma(reason="the diagonal's elements lie apart"):
                    row = GB * GR
                    for r in range(GB):
                        src = bass.AP(adj_t.tensor, r * (GR + P), [[row + 1, P], [(NC + 1) * P * row, NG]])
                        act.dma_start(diag[:, :].rearrange("p (q r) -> p q r", r=GB)[:, :, r], src)\
                            .then_inc(diag_loaded, 16)
                act.dma_start(bg[:, :], bias_g[0:1, :].to_broadcast([P, F])).then_inc(b_loaded, 16)
                act.dma_start(b2[:, :], bias_2[0:1, :].to_broadcast([P, F])).then_inc(b_loaded, 16)

            def hi_of_weights(part, loaded, count):
                act.wait_ge(loaded, count)
                nc.scalar.activation(wsp[:, 0, part], shared[:, part], ACT.Copy, scale=W_SCALE).then_inc(w_hi, 1)

            def split(p, g, c):
                act.wait_ge(adj_loaded[c % 2], at(PLAIN, p, g, 16 * NC // 2, (c // 2 + 1) * 16))
                first = isinstance(g, int) and g == 0
                if c >= 2:
                    act.wait_ge(chunk_done, at(PLAIN, p, g, NC - 1, c - 1))
                elif not (first and p == 0):
                    if c == 1:
                        act.wait_ge(acc_ready, at(ALL, p, g, GB, 0))
                    elif first and p == ATT + 1:
                        act.wait_ge(block_done, (NB - 1) * (NG - 1) + NB - GB)
                    else:
                        act.wait_ge(chunk_done, at(PLAIN, p, g, NC - 1, 0))
                nc.scalar.activation(ahi[:, c % 2, :, :], adj[:, c % 2, :, :], ACT.Copy, scale=ADJ_SCALE)\
                    .then_inc(split_hi, 1)

            def ev_used(p, g):
                if p in SELF:
                    act.wait_ge(sum_ready, at(SELF, p, g))
                    if p == 0:
                        act.wait_ge(row_ready, at([0], p, g, 2, 2))
                elif p in SCALED:
                    act.wait_ge(scaled, at(SCALED, p, g, GB, GB))
                else:
                    act.wait_ge(preact, at([4, 5], p, g))

            def evacuate(p, g):
                if not isinstance(g, int) or g > 0:
                    ev_used(p, g - 1)
                elif p > 0:
                    ev_used(p - 1, NG - 1)
                n = F + 1 if p in (0, ATT) else F
                for b in range(GB):
                    act.wait_ge(acc_ready, at(ALL, p, g, GB, b + 1))
                    nc.scalar.activation(ev[:, b, 0:n], acc[:, b, 0:n], ACT.Copy,
                                         scale=1.0 if p == ATT else 1.0 / ADJ_SCALE).then_inc(ev_ready, 1)

            def blocks(g, b, n=1):
                return bass.ds(g * GB + b, n)

            def hi_of_t(p, g):
                act.wait_ge(sum_ready, at(SELF, p, g))
                act.wait_ge(d_ready, 1)
                for b in range(GB):
                    nc.scalar.activation(mov[1][:, blocks(g, b), 0:F], o[:, b, :], ACT.Copy, scale=d[:, blocks(g, b)])\
                        .then_inc(mov_hi, 1)

            def hi_of_h(p, g):
                o, hsp, u = work(p, g)
                if p == 4:
                    act.wait_ge(preact, at([4, 5], p, g))
                else:
                    act.wait_ge(shift_ready, at(NORM, p, g))
                if p == PRE:
                    if g >= 2:
                        act.wait_ge(h_turned, at(SMALL, p, g - 2, 2, 2))
                elif not isinstance(g, int) or g > 0:
                    act.wait_ge(h_turned, at(SMALL, p, g - 1, 2, 2))
                    if p == 1:
                        act.wait_ge(gn_turned, at([1], p, g - 1, 2, 2))
                else:
                    act.wait_ge(h_turned, at(SMALL, SMALL[SMALL.index(p) - 1], NG - 1, 2, 2))
                    if p == 2:
                        act.wait_ge(gn_turned, at([1], 1, NG - 1, 2, 2))
                if p == 4:
                    nc.scalar.activation(hsp[:, 0, :, :], o[:, :, :], ACT.Relu).then_inc(h_hi, GB)
                else:
                    for b in range(GB):
                        nc.scalar.activation(hsp[:, 0, b, :], xres[:, blocks(g, b), :].rearrange("p a n -> p (a n)"),
                                             ACT.Relu, bias=shift[:, u, b:b + 1], scale=rstd[:, u, b:b + 1])\
                            .then_inc(h_hi, 1)

            def keep_hT(p, g, r):
                act.wait_ge(h_turned, at(SMALL, p, g, 2, r + 1))
                if not isinstance(g, int) or g > 0:
                    act.wait_ge(small_ready, at(SMALL, p, g - 1, 2, r + 1))
                elif p > PRE:
                    act.wait_ge(small_ready, at(SMALL, SMALL[SMALL.index(p) - 1], NG - 1, 2, r + 1))
                nc.scalar.activation(hT[:, :, 2 * P * r:2 * P * (r + 1)],
                                     (psT2 if p == PRE and r == 1 else psT)[:, :, :], ACT.Copy)\
                    .then_inc(hT_ready, 1)

            def small_out(p, b):
                return small_bank(p, b)[:, -F:]

            def hi_of_small(p, g, r):
                act.wait_ge(small_ready, at(SMALL, p, g, 2, r + 1))
                for b in (2 * r, 2 * r + 1):
                    if p in DIRECT:
                        nc.scalar.activation(direct[:, blocks(g, b), :], small_bank(p, b)[:, 0:F], ACT.Copy, scale=1.0 / W_SCALE)\
                            .then_inc(direct_ready, 1)
                    if p == 1:
                        nc.scalar.activation(junk[:, b, :], small_out(p, b), ACT.Square, scale=1.0 / W_SCALE,
                                             accum_out=ssq[:, b:b + 1]).then_inc(ssq_ready, 1)
                    nc.scalar.activation(mov[(p + 1) % 2][:, blocks(g, b), 0:F], small_out(p, b), ACT.Copy,
                                         scale=dinv_w[:, blocks(g, b)] if p == 2 else 1.0 / W_SCALE)\
                        .then_inc(mov_hi, 1)

            def hi_of_gn(p, g, r):
                act.wait_ge(rnorm_ready, at([1], p, g, 2, r + 1))
                act.wait_ge(mov_ready, at(MOVE, p, g, GB, 2 * r + 2))
                act.wait_ge(h_turned, at(SMALL, p, g, 2, r + 1))
                for b in (2 * r, 2 * r + 1):
                    nc.scalar.activation(hsp[:, 0, b, :], small_out(p, b), ACT.Copy, scale=rnorm[:, b:b + 1])\
                        .then_inc(gn_hi, 1)

            def keep_gnT(p, g, r):
                act.wait_ge(gn_turned, at([1], p, g, 2, r + 1))
                nc.scalar.activation(gnT[:, :, bass.ds(g * GR + 2 * P * r, 2 * P)], psT[:, :, :], ACT.Copy)\
                    .then_inc(gnT_ready, 1)

            def stage(name, p, g):
                if name == "ev":
                    evacuate(p, g)
                elif name == "h":
                    if p == 0:
                        hi_of_t(p, g)
                    elif p in SMALL:
                        hi_of_h(p, g)
                elif p in SMALL and name == "T0":
                    keep_hT(p, g, 0)
                elif p in SMALL and name == "W0":
                    hi_of_small(p, g, 0)
                elif p in SMALL and name == "T1":
                    keep_hT(p, g, 1)
                elif p in SMALL and name == "W1":
                    hi_of_small(p, g, 1)
                elif p == 1 and name in ("n0", "n1"):
                    hi_of_gn(p, g, int(name[1]))
                elif p == 1 and name in ("g0", "g1"):
                    keep_gnT(p, g, int(name[1]))

            PLACES = {0: ["ev"], 3: ["h"], 4: ["T0"], 5: ["W0", "T1", "n0"], 6: ["W1", "n1"], 7: ["g0", "g1"]}
            ATT_PLACES = [{2: ["ev"], 10: ["h"], 14: ["T0"], 16: ["W0", "T1"], 17: ["n0"], 19: ["W1"],
                           20: ["n1"], 22: ["g0"], 24: ["g1"]},
                          {2: ["ev"], 17: ["h"], 23: ["T0"], 26: ["W0", "T1"], 30: ["W1"]}]

            def group(p, g, tp, tg):
                for c in range(NC):
                    split(p, g, c)
                    for name in PLACES.get(c, []):
                        stage(name, tp, tg)

            def exponential(g, j):
                H = j // HALF
                if j % HALF == 0:
                    exp_slot_free(act, g, H)
                act.wait_ge(sim_ready, g * NB + j + 1)
                nc.scalar.activation(expo[:, H % 4, (j % HALF) * GR:(j % HALF + 1) * GR], psS[:, j % 2, :], ACT.Exp,
                                     scale=1.0 / (GN_SCALE * GN_SCALE)).then_inc(exp_ready, 1)

            def hi_of_numerators(g, j):
                n = g * NB + j
                act.wait_ge(num_ready, n + 1)
                if n == 0:
                    act.wait_ge(chunk_done, 2 * NG * (NC - 1))
                elif n == GB:
                    act.wait_ge(acc_ready, 2 * NG * GB)
                elif n >= 2 * GB:
                    if (n - 2 * GB) % NB == NB - 1:
                        act.wait_ge(acc_ready, at(ALL, ATT, g, GB, 0))
                    else:
                        before = n - 2 * GB
                        act.wait_ge(block_done, before // NB * (NB - 1) + before % NB + 1)
                nc.scalar.activation(ahi[:, (j // GB) % 2, j % GB, :], nums[:, n % NUMS, :], ACT.Copy, scale=P_SCALE)\
                    .then_inc(num_hi, 1)

            def att_group(g, tp, tg):
                for j in range(NB):
                    if computed(g, j):
                        exponential(g, j)
                    if j > 0:
                        hi_of_numerators(g, j - 1)
                    elif g > 0:
                        hi_of_numerators(g - 1, NB - 1)
                    for name in ATT_PLACES[g > 0].get(j, []):
                        stage(name, tp, tg)

            stage("h", PRE, 0)
            hi_of_weights(slice(0, wofs[1]), w0_loaded, 16)
            for q in range(NG):
                for name in ["T0", "T1", "W0"]:
                    stage(name, PRE, q)
                if q + 1 < NG:
                    stage("h", PRE, q + 1)
                stage("W1", PRE, q)
                split(0, 0, q)
                if q == 1:
                    load_others()
            hi_of_weights(slice(wofs[1], wofs[5]), w_loaded, 16 * 4)
            for p in range(6):
                if p == ATT:
                    act.wait_ge(dinv_ready, 2 * NG)
                    for g in range(NG):
                        att_group(g, *((ATT, g - 1) if g else (1, NG - 1)))
                    hi_of_numerators(NG - 1, NB - 1)
                else:
                    if p > 0:
                        group(p, 0, p - 1, NG - 1)
                    with act.Fori(1, NG) as g:
                        group(p, g, p, g - 1)
            stage("ev", 5, NG - 1)

        @block.vector
        def _(dve):
            for i in range(2):
                nc.vector.memset(mov[i][:, :, F:LO], 1.0).then_inc(ones_ready, 1)

            def blocks(g, b, n=1):
                return bass.ds(g * GB + b, n)

            def split(p, g, c):
                dve.wait_ge(split_hi, chunk_no(p, g, c) + 1)
                nc.vector.scalar_tensor_tensor(alo[:, c % 2, :, :].rearrange("p b n -> p (b n)"),
                                               adj[:, c % 2, :, :].rearrange("p b n -> p (b n)"), ADJ_SCALE,
                                               ahi[:, c % 2, :, :].rearrange("p b n -> p (b n)"),
                                               ALU.mult, ALU.subtract).then_inc(split_ready, 1)

            def epilogue(p, g):
                dve.wait_ge(ev_ready, at(ALL, p, g, GB, GB))
                if p in SELF:
                    dve.wait_ge(own_ready, at(SELF, p, g))
                    nc.vector.tensor_tensor(o[:, :, :], ev[:, :, 0:F], own[:, :, :], ALU.add)\
                        .then_inc(sum_ready, 1)
                    if p == 0:
                        nc.vector.tensor_scalar(rowm[:, :], ev[:, :, F], 0.0, None, ALU.is_gt)\
                            .then_inc(row_ready, 1)
                        nc.vector.tensor_scalar(rowc[:, :], ev[:, :, F], TINY, None, ALU.max).then_inc(row_ready, 1)
                    dve.wait_ge(sum_ready, at(SELF, p, g))
                if p == 0:
                    return
                if p == 1:
                    for b in range(GB):
                        nc.vector.tensor_scalar(o[:, b, :], o[:, b, :], d[:, blocks(g, b)], None, ALU.mult)\
                            .then_inc(scaled, 1)
                elif p == 2:
                    nc.vector.reciprocal(rden[:, :], ev[:, :, F]).then_inc(den_ready, 1)
                    dve.wait_ge(den_ready, at([2], p, g))
                    for b in range(GB):
                        nc.vector.scalar_tensor_tensor(o[:, b, :], ev[:, b, 0:F], rden[:, b:b + 1], bg[:, :],
                                                       ALU.mult, ALU.add).then_inc(scaled, 1)
                elif p == 3:
                    for b in range(GB):
                        nc.vector.scalar_tensor_tensor(o[:, b, :], ev[:, b, 0:F], dinv[:, blocks(g, b)], b2[:, :],
                                                       ALU.mult, ALU.add).then_inc(scaled, 1)
                else:
                    dve.wait_ge(direct_ready, at(DIRECT, p - 1, g, GB, GB))
                    nc.vector.tensor_tensor(o[:, :, :], ev[:, :, 0:F], direct[:, blocks(g, 0, GB), :], ALU.add)\
                        .then_inc(preact, 1)

            def residual(p, g):
                rows = xres[:, blocks(g, 0, GB), :]
                if p in SCALED:
                    dve.wait_ge(scaled, at(SCALED, p, g, GB, GB))
                elif p == 5:
                    dve.wait_ge(preact, at([4, 5], p, g))
                if p == 2:
                    nc.vector.tensor_tensor(rows, o[:, :, :], rows, ALU.add).then_inc(x_ready, 1)
                elif p in RES:
                    nc.vector.scalar_tensor_tensor(rows, o[:, :, :], 0.0, rows, ALU.max, ALU.add).then_inc(x_ready, 1)

            def norm_stats(p, g):
                if p == PRE:
                    dve.wait_ge(x_loaded[g], 16)
                else:
                    dve.wait_ge(x_ready, at(RES, p, g))
                dve.sem_inc(passed, 1)
                u = work(p, g)[2]
                for b in range(GB):
                    nc.vector.bn_stats(stats[:, b, :], xres[:, blocks(g, b), :].rearrange("p a n -> p (a n)"))\
                        .then_inc(stats_ready, 1)
                dve.wait_ge(stats_ready, at(NORM, p, g, GB, GB))
                dve.sem_inc(passed, 1)
                for b in range(GB):
                    nc.vector.bn_aggr(mv[:, u, b, :], stats[:, b, :]).then_inc(mv_ready, 1)
                dve.wait_ge(mv_ready, at(NORM, p, g, GB, GB))
                nc.vector.tensor_scalar(nmean[:, u, :], mv[:, u, :, 0], -1.0, None, ALU.mult).then_inc(var_ready, 1)
                nc.vector.tensor_scalar(vare[:, u, :], mv[:, u, :, 1], LN_EPS, None, ALU.add).then_inc(var_ready, 1)

            def normalise(p, g):
                o, _, u = work(p, g)
                dve.wait_ge(rstd_ready, at(NORM, p, g))
                for b in range(GB):
                    nc.vector.tensor_scalar(o[:, b, :], xres[:, blocks(g, b), :].rearrange("p a n -> p (a n)"),
                                            mv[:, u, b, 0:1], rstd[:, u, b:b + 1], ALU.subtract, ALU.mult)\
                        .then_inc(normed, 1)

            def lo_of_h(p, g):
                o, hsp, _ = work(p, g)
                if p in NORM:
                    dve.wait_ge(normed, at(NORM, p, g, GB, GB))
                dve.wait_ge(h_hi, at(SMALL, p, g, GB, GB))
                nc.vector.scalar_tensor_tensor(hsp[:, 1, :, :], o[:, :, :], 0.0, hsp[:, 0, :, :],
                                               ALU.max, ALU.subtract).then_inc(h_ready, 1)

            def lo_of_t(p, g):
                for b in range(GB):
                    dve.wait_ge(mov_hi, at(MOVE, p, g, GB, b + 1))
                    nc.vector.scalar_tensor_tensor(mov[1][:, blocks(g, b), LO:MW], o[:, b, :], d[:, blocks(g, b)],
                                                   mov[1][:, blocks(g, b), 0:F], ALU.mult, ALU.subtract)\
                        .then_inc(mov_ready, 1)
                dve.wait_ge(rowp_ready, at([0], p, g))
                nc.vector.tensor_tensor(dinv[:, blocks(g, 0, GB)], rowp[:, :], rowm[:, :], ALU.mult)\
                    .then_inc(dinv_ready, 1)
                nc.vector.scalar_tensor_tensor(dinv_w[:, blocks(g, 0, GB)], rowp[:, :], 1.0 / W_SCALE, rowm[:, :],
                                               ALU.mult, ALU.mult).then_inc(dinv_ready, 1)

            def small_out(p, b):
                return small_bank(p, b)[:, -F:]

            def lo_of_small(p, g, r):
                for b in (2 * r, 2 * r + 1):
                    dve.wait_ge(mov_hi, at(MOVE, p, g, GB, b + 1 if p in DIRECT else 2 * r + 2))
                    m = mov[(p + 1) % 2]
                    nc.vector.scalar_tensor_tensor(m[:, blocks(g, b), LO:MW], small_out(p, b),
                                                   dinv_w[:, blocks(g, b)] if p == 2 else 1.0 / W_SCALE,
                                                   m[:, blocks(g, b), 0:F], ALU.mult, ALU.subtract)\
                        .then_inc(mov_ready, 1)

            def guard_norm(p, g, r):
                dve.wait_ge(ssq_ready, at([1], p, g, GB, 2 * r + 2))
                nc.vector.tensor_scalar(ssqc[:, 2 * r:2 * r + 2], ssq[:, 2 * r:2 * r + 2], NORM_EPS * NORM_EPS, None,
                                        ALU.max).then_inc(ssqc_ready, 1)

            def lo_of_gn(p, g, r):
                for b in (2 * r, 2 * r + 1):
                    dve.wait_ge(gn_hi, at([1], p, g, GB, 2 * r + 2))
                    nc.vector.scalar_tensor_tensor(hsp[:, 1, b, :], small_out(p, b), rnorm[:, b:b + 1],
                                                   hsp[:, 0, b, :], ALU.mult, ALU.subtract).then_inc(gn_ready, 1)

            def stage(name, p, g):
                if name == "epi":
                    epilogue(p, g)
                elif name == "x" and p in RES:
                    residual(p, g)
                elif name == "norm" and p in NORM:
                    normalise(p, g)
                elif name == "stats" and p in NORM:
                    norm_stats(p, g)
                elif name == "h":
                    if p == 0:
                        lo_of_t(p, g)
                    elif p in SMALL:
                        lo_of_h(p, g)
                elif p in SMALL and name == "W0":
                    if p == 1:
                        guard_norm(p, g, 0)
                    lo_of_small(p, g, 0)
                elif p in SMALL and name == "W1":
                    if p == 1:
                        guard_norm(p, g, 1)
                    lo_of_small(p, g, 1)
                elif p == 1 and name in ("n0", "n1"):
                    lo_of_gn(p, g, int(name[1]))

            PLACES = {1: ["epi"], 2: ["x", "stats"], 3: ["norm", "h"], 5: ["W0", "n0"], 6: ["W1", "n1"]}
            ATT_PLACES = [{4: ["epi"], 6: ["x"], 7: ["stats"], 9: ["norm"], 10: ["h"], 16: ["W0"], 17: ["n0"],
                           19: ["W1"], 20: ["n1"]},
                          {4: ["epi"], 8: ["x"], 11: ["stats"], 14: ["norm"], 17: ["h"], 26: ["W0"], 30: ["W1"]}]

            def group(p, g, tp, tg):
                for c in range(NC):
                    split(p, g, c)
                    for name in PLACES.get(c, []):
                        stage(name, tp, tg)

            def numerators(g, j):
                n, H = g * NB + j, j // HALF
                if j % HALF == 0:
                    dve.wait_ge(half_loaded[H % 4], 16 * (g * NH // 4 + H // 4 + 1))
                if n >= NUMS:
                    dve.wait_ge(num_split, n - NUMS + 1)
                if computed(g, j):
                    dve.wait_ge(exp_ready, exp_no(g, j))
                    e = expo[:, H % 4, (j % HALF) * GR:(j % HALF + 1) * GR]
                else:
                    dve.wait_ge(sim_ready, n + 1)
                    e = psS[:, j % 2, :]
                nc.vector.scalar_tensor_tensor(nums[:, n % NUMS, :], adj[:, (j // GB) % 2, j % GB, :], ADJ_EPS, e,
                                               ALU.add, ALU.mult).then_inc(num_ready, 1)

            def lo_of_numerators(g, j):
                n = g * NB + j
                dve.wait_ge(num_hi, n + 1)
                nc.vector.scalar_tensor_tensor(alo[:, (j // GB) % 2, j % GB, :], nums[:, n % NUMS, :], P_SCALE,
                                               ahi[:, (j // GB) % 2, j % GB, :], ALU.mult, ALU.subtract)\
                    .then_inc(num_split, 1)

            def att_group(g, tp, tg):
                for j in range(NB):
                    numerators(g, j)
                    if j > 0:
                        lo_of_numerators(g, j - 1)
                    elif g > 0:
                        lo_of_numerators(g - 1, NB - 1)
                    for name in ATT_PLACES[g > 0].get(j, []):
                        stage(name, tp, tg)

            def lo_of_weights(part, n):
                dve.wait_ge(w_hi, n)
                nc.vector.scalar_tensor_tensor(wsp[:, 1, part], shared[:, part], W_SCALE, wsp[:, 0, part],
                                               ALU.mult, ALU.subtract).then_inc(w_ready, 1)

            for name, q in [("stats", 0), ("norm", 0), ("stats", 1), ("h", 0)]:
                stage(name, PRE, q)
            lo_of_weights(slice(0, wofs[1]), 1)
            for q in range(NG):
                if q + 1 < NG:
                    stage("norm", PRE, q + 1)
                if q + 2 < NG:
                    stage("stats", PRE, q + 2)
                stage("W0", PRE, q)
                if q + 1 < NG:
                    stage("h", PRE, q + 1)
                stage("W1", PRE, q)
                split(0, 0, q)
            lo_of_weights(slice(wofs[1], wofs[5]), 2)
            dve.wait_ge(diag_loaded, 16 * GB)
            nc.vector.tensor_scalar(diag[:, :], diag[:, :], 1.0, None, ALU.add).then_inc(diag_one, 1)
            dve.wait_ge(b_loaded, 32)
            for p in range(6):
                if p == ATT:
                    dve.wait_ge(dinv_ready, 2 * NG)
                    for g in range(NG):
                        att_group(g, *((ATT, g - 1) if g else (1, NG - 1)))
                    lo_of_numerators(NG - 1, NB - 1)
                else:
                    if p > 0:
                        group(p, 0, p - 1, NG - 1)
                    with dve.Fori(1, NG) as g:
                        group(p, g, p, g - 1)
            dve.wait_ge(direct_ready, at(DIRECT, 4, NG - 1, GB, GB))
            for b in range(GB):
                j = (NG - 1) * GB + b
                dve.wait_ge(ev_ready, at(ALL, 5, NG - 1, GB, b + 1))
                nc.vector.tensor_tensor(o[:, b, :], ev[:, b, 0:F], direct[:, j, :], ALU.add).then_inc(preact, 1)
                dve.wait_ge(preact, at([4, 5], 5, NG - 1, 1, b + 1))
                nc.vector.scalar_tensor_tensor(xres[:, j, :], o[:, b, :], 0.0, xres[:, j, :], ALU.max, ALU.add)\
                    .then_inc(x_ready, 1)


def kernel(x, adj, L0_gnn_W, L1_gnn_weight, L1_gnn_bias, L2_gnn_W, L2_gnn_b, L3_gnn_W1, L3_gnn_W2):
    import concourse.bacc as bacc
    from concourse.bass_utils import run_bass_kernel_spmd

    def rows_on_partitions(w):
        return w.reshape(-1, P, w.shape[1]).transpose(1, 0, 2)

    def halves(w):
        return rows_on_partitions(np.concatenate([w[:F], w[F:]], axis=1))

    arrays = {
        "x": np.asarray(x).reshape(NG, GB, P, F).transpose(0, 2, 1, 3).reshape(NG * P, GB * F),
        "adj_t": np.asarray(adj).reshape(NG, GR, NC, GB, P).transpose(0, 2, 4, 3, 1).reshape(NG * NC * P, GB * GR),
        "w0": rows_on_partitions(np.asarray(L0_gnn_W).T),
        "wg": rows_on_partitions(np.asarray(L1_gnn_weight)),
        "bias_g": np.asarray(L1_gnn_bias).reshape(1, F),
        "w2": rows_on_partitions(np.asarray(L2_gnn_W)),
        "bias_2": np.asarray(L2_gnn_b).reshape(1, F),
        "w3a": halves(np.asarray(L3_gnn_W1)),
        "w3b": halves(np.asarray(L3_gnn_W2)),
    }
    nc = bacc.Bacc("TRN2", target_bir_lowering=False, num_devices=1, dynamic_dma_scratch_size=1024)
    aps = {}
    for name, a in arrays.items():
        arrays[name] = np.ascontiguousarray(a)
        aps[name] = nc.dram_tensor(f"in_{name}", a.shape, mybir.dt.from_np(a.dtype), kind="ExternalInput").ap()
    out = nc.dram_tensor("out", (N, F), mybir.dt.float32, kind="ExternalOutput").ap()
    sent = nc.dram_tensor("sent", (NC * (NC - 1) * P, 2 * GR), mybir.dt.float32, kind="Internal").ap()
    build(nc, sent=sent, out=out, **aps)
    r = run_bass_kernel_spmd(nc, [{f"in_{name}": a for name, a in arrays.items()}], core_ids=[0])
    return r.results[0]["out"]
```

```python
from contextlib import ExitStack

import concourse.bass as bass
import numpy as np
from concourse import mybir

N = 4096
F = 256
P = 128
NB = N // P
GB = 4
NG = NB // GB
NC = NB // GB
GR = GB * P
FB = F // P
LO = F + 2
MW = 2 * LO
LN_EPS = 1e-5
ADJ_EPS = 1e-8
NORM_EPS = 1e-8
TINY = 1.2e-38
ADJ_SCALE = 256.0
W_SCALE = 64.0
P_SCALE = 4096.0
GN_SCALE = 64.0
WARM = [60, 60]
LEAD = 3
HALF = GB // 2
NH = NB // HALF
NUMS = 3
PRE = -1
ATT = 2
TURNED = 4


def build(nc, x, adj_t, w0, wg, bias_g, w2, bias_2, w3a, w3b, sent, out):
    f32, f16 = mybir.dt.float32, mybir.dt.float16
    ALU, ACT = mybir.AluOpType, mybir.ActivationFunctionType

    ctx = ExitStack()
    with ctx:
        def sb(name, shape, dt):
            return ctx.enter_context(nc.sbuf_tensor(name, shape, dt))

        def pb(name, shape, dt):
            return ctx.enter_context(nc.psum_tensor(name, shape, dt))

        def sem(name):
            return ctx.enter_context(nc.semaphore(name))

        xres = sb("xres", [P, NB, F], f32)
        mov = [sb(f"mov{i}", [P, NB, MW], f16) for i in range(2)]
        shared = sb("shared", [P, 2 * FB * N // 2], f32)
        gnT = shared[:, :].bitcast(f16).rearrange("p (q n) -> p q n", q=2 * FB)
        direct = shared[:, :].rearrange("p (b n) -> p b n", n=F)
        directT = shared[:, :].rearrange("p (q n) -> p q n", n=GR)
        wcols = [F, F, F, 2 * F, 2 * F]
        wofs = [sum(wcols[:i]) * FB for i in range(6)]
        wraw = [shared[:, wofs[i]:wofs[i + 1]].rearrange("p (f n) -> p f n", f=FB) for i in range(5)]
        wsp = sb("wsp", [P, 2, wofs[5]], f16)
        wpart = [[wsp[:, s, wofs[i]:wofs[i + 1]].rearrange("p (f n) -> p f n", f=FB) for s in range(2)]
                 for i in range(5)]
        weights_of = {PRE: wpart[0], 1: wpart[1], 2: wpart[2], 3: wpart[3], 4: wpart[4]}
        adj = sb("adj", [P, 2, GB, GR], f32)
        ahi = sb("ahi", [P, 2, GB, GR], f16)
        alo = sb("alo", [P, 2, GB, GR], f16)
        expo = sb("expo", [P, 4, HALF * GR], f32)
        nums = sb("nums", [P, NUMS, GR], f32)
        ev = sb("ev", [P, GB, F + 1], f32)
        o = sb("o", [P, GB, F], f32)
        oT = o[:, :, :].rearrange("p b n -> p (b n)").rearrange("p (f n) -> p f n", f=FB)
        hsp = sb("hsp", [P, 2, GB, F], f16)
        o2 = expo[:, 0, :].rearrange("p (b n) -> p b n", b=GB)
        hsp2 = expo[:, 1, :].bitcast(f16).rearrange("p (s b n) -> p s b n", s=2, b=GB)
        own = sb("own", [P, GB, F], f32)
        hT = sb("hT", [P, 2 * FB, GR], f16)
        bg = sb("bg", [P, F], f32)
        b2 = sb("b2", [P, F], f32)
        ident = sb("ident", [P, P], f16)
        ident32 = sb("ident32", [P, P], f32)
        diag = sb("diag", [P, NB], f32)
        d = sb("d", [P, NB], f32)
        dinv = sb("dinv", [P, NB], f32)
        dinv_w = sb("dinv_w", [P, NB], f32)
        neghalf = sb("neghalf", [P, NB], f32)
        stats = sb("stats", [P, GB, 6], f32)
        mv = sb("mv", [P, 2, GB, 2], f32)
        vare = sb("vare", [P, 2, GB], f32)
        rstd = sb("rstd", [P, 2, GB], f32)
        nmean = sb("nmean", [P, 2, GB], f32)
        shift = sb("shift", [P, 2, GB], f32)
        rowc = sb("rowc", [P, GB], f32)
        rowm = sb("rowm", [P, GB], f32)
        rowp = sb("rowp", [P, GB], f32)
        rden = sb("rden", [P, GB], f32)
        ssq = sb("ssq", [P, GB], f32)
        ssqc = sb("ssqc", [P, GB], f32)
        rnorm = sb("rnorm", [P, GB], f32)
        junk = sb("junk", [P, GB, F], f16)

        acc = pb("acc", [P, GB, GR], f32)
        psT = pb("psT", [P, 2 * FB, 2 * P], f16)
        psW = pb("psW", [P, 2 * F], f32)
        psS = pb("psS", [P, 2, GR], f32)
        psT2 = psS[:, 0, :].bitcast(f16).rearrange("p (q n) -> p q n", q=2 * FB)

        w0_loaded = sem("w0_loaded")
        w_loaded = sem("w_loaded")
        b_loaded = sem("b_loaded")
        diag_loaded = sem("diag_loaded")
        x_loaded = [sem(f"x_loaded{q}") for q in range(NG)]
        adj_loaded = [sem(f"adj_loaded{s}") for s in range(2)]
        half_loaded = [sem(f"half_loaded{q}") for q in range(4)]
        exp_sent = [sem(f"exp_sent{q}") for q in range(4)]
        exp_back = [sem(f"exp_back{q}") for q in range(4)]
        stored = sem("stored")
        const_ready = sem("const_ready")
        ident_zero = sem("ident_zero")
        ones_ready = sem("ones_ready")
        w_hi = sem("w_hi")
        w_ready = sem("w_ready")
        diag_one = sem("diag_one")
        d_ready = sem("d_ready")
        split_hi = sem("split_hi")
        split_ready = sem("split_ready")
        chunk_done = sem("chunk_done")
        exp_ready = sem("exp_ready")
        sim_ready = sem("sim_ready")
        num_ready = sem("num_ready")
        num_hi = sem("num_hi")
        num_split = sem("num_split")
        block_done = sem("block_done")
        acc_ready = sem("acc_ready")
        cross_ready = sem("cross_ready")
        ev_ready = sem("ev_ready")
        own_ready = sem("own_ready")
        sum_ready = sem("sum_ready")
        row_ready = sem("row_ready")
        rowp_ready = sem("rowp_ready")
        dinv_ready = sem("dinv_ready")
        den_ready = sem("den_ready")
        scaled = sem("scaled")
        preact = sem("preact")
        x_ready = sem("x_ready")
        stats_ready = sem("stats_ready")
        passed = sem("passed")
        mv_ready = sem("mv_ready")
        var_ready = sem("var_ready")
        rstd_ready = sem("rstd_ready")
        shift_ready = sem("shift_ready")
        normed = sem("normed")
        h_hi = sem("h_hi")
        h_ready = sem("h_ready")
        h_turned = sem("h_turned")
        hT_ready = sem("hT_ready")
        small_ready = sem("small_ready")
        direct_ready = sem("direct_ready")
        mov_hi = sem("mov_hi")
        mov_ready = sem("mov_ready")
        ssq_ready = sem("ssq_ready")
        ssqc_ready = sem("ssqc_ready")
        rnorm_ready = sem("rnorm_ready")
        gn_hi = sem("gn_hi")
        gn_ready = sem("gn_ready")
        gn_turned = sem("gn_turned")
        gnT_ready = sem("gnT_ready")

        ALL = [0, 1, 2, 3, 4, 5]
        NORM = [PRE, 1, 2, 3]
        SMALL = [PRE, 1, 2, 3, 4]
        SELF = [0, 1]
        RES = [1, 2, 3, 5]
        SCALED = [1, 2, 3]
        DIRECT = [3, 4]
        MOVE = [PRE, 0, 1, 2, 3, 4]

        def at(passes, p, g, per=1, k=1):
            return (g + NG * passes.index(p)) * per + k

        CROSS = [1, 3, 5]
        PLAIN = [0, 1, 3, 4, 5]

        def chunk_no(p, g, c):
            return (g + NG * PLAIN.index(p)) * NC + c

        def computed(g, j):
            return j >= GB * g

        def turned(g, j):
            return GB if j < GB * g else (j - GB * g if j < GB * (g + 1) else 0)

        def is_sent(g, H):
            return H >= NH // NC * (g + 1)

        def exp_no(g, j):
            return sum(NB - GB * h for h in range(g)) + j - GB * g + 1

        def sent_no(g, H):
            return sum(is_sent(a, b) and b % 4 == H % 4 and (a, b) <= (g, H) for a in range(NG) for b in range(NH))

        def back_no(g, H):
            return sum(not computed(a, HALF * b) and b % 4 == H % 4 and (a, b) <= (g, H)
                       for a in range(NG) for b in range(NH))

        def exp_slot_free(eng, g, H):
            g, H = (g, H - 4) if H >= 4 else (g - 1, H - 4 + NH)
            if g < 0:
                return
            if computed(g, HALF * H):
                eng.wait_ge(num_ready, g * NB + (GB * (g + 1) if turned(g, HALF * H + 1) else HALF * (H + 1)))
                if is_sent(g, H):
                    eng.wait_ge(exp_sent[H % 4], 32 * sent_no(g, H))
            else:
                eng.wait_ge(sim_ready, g * NB + HALF * (H + 1))

        def exp_of(j):
            return expo[:, j // HALF % 4, j % HALF * GR:(j % HALF + 1) * GR]

        def sent_rows(g, c):
            return 2 * P * (sum(NC - 1 - h for h in range(g)) + c - g - 1)

        def work(p, g):
            return (o2, hsp2, 1) if p == PRE and g % 2 else (o, hsp, 0)

        def small_bank(p, b):
            if p == TURNED:
                return psW[:, :] if b % 2 == 0 else psS[:, 0, :]
            bank = psS[:, 0, :] if p == 3 else psS[:, 1, :] if p == PRE and b >= 2 else psW
            return bank[:, (b % 2) * F:(b % 2 + 1) * F]

        block = ctx.enter_context(nc.Block())

        @block.sync
        def _(sp):
            def load_x(q):
                sp.dma_start(xres[:, GB * q:GB * (q + 1), :].rearrange("p b n -> p (b n)"),
                             x[q * P:(q + 1) * P, :]).then_inc(x_loaded[q], 16)

            def load(p, g, c, first=False):
                if not first:
                    q, h, e = (p, g, c - 2) if c >= 2 else ((p, g - 1, c + 6) if not isinstance(g, int) or g > 0
                                                            else (p - 1, NG - 1, c + 6))
                    if q == ATT:
                        sp.wait_ge(num_ready, h * NB + GB * (e + 1))
                    else:
                        sp.wait_ge(split_ready, chunk_no(q, h, e) + 1)
                row = g * (NC * P) + c * P
                sp.dma_start(adj[:, c % 2, :, :].rearrange("p b n -> p (b n)"), adj_t[bass.ds(row, P), :])\
                    .then_inc(adj_loaded[c % 2], 16)

            def store(g):
                sp.wait_ge(x_ready, at(RES, 5, g))
                sp.dma_start(out[bass.ds(g * GR, GR), :].rearrange("(b p) n -> p b n", p=P),
                             xres[:, bass.ds(g * GB, GB), :]).then_inc(stored, 16)

            def load_others():
                for src, dst in zip([wg, w2, w3a, w3b], wraw[1:]):
                    sp.dma_start(dst, src).then_inc(w_loaded, 16)
                with nc.allow_non_contiguous_dma(reason="the diagonal's elements lie apart"):
                    row = GB * GR
                    for r in range(GB):
                        src = bass.AP(adj_t.tensor, r * (GR + P), [[row + 1, P], [(NC + 1) * P * row, NG]])
                        sp.dma_start(diag[:, :].rearrange("p (q r) -> p q r", r=GB)[:, :, r], src)\
                            .then_inc(diag_loaded, 16)
                sp.dma_start(bg[:, :], bias_g[0:1, :].to_broadcast([P, F])).then_inc(b_loaded, 16)
                sp.dma_start(b2[:, :], bias_2[0:1, :].to_broadcast([P, F])).then_inc(b_loaded, 16)

            def group(p, g, first=False):
                for c in range(2 if first else 0, NC):
                    load(p, g, c)
                    if first and c == 3:
                        load_others()
                    if p == 5 and c == 5 and not isinstance(g, int):
                        store(g - 1)

            def send(g, H):
                sp.wait_ge(exp_ready, exp_no(g, HALF * H + HALF - 1))
                k = H % 2 * HALF
                rows = sent_rows(g, H // 2)
                to = sent[rows:rows + 2 * P, k * GR // 2:(k + HALF) * GR // 2]
                for e in range(2):
                    sp.dma_start(to[e * P:(e + 1) * P, :].rearrange("p (b n) -> p b n", b=HALF),
                                 expo[:, H % 4, :].rearrange("p (b n) -> p b n", b=HALF)[:, :, e * GR // 2:(e + 1) * GR // 2])\
                        .then_inc(exp_sent[H % 4], 16)

            def att_half(g, H):
                c = H // 2
                if g == 0 and H < 4:
                    sp.wait_ge(split_ready, chunk_no(ATT - 1, NG - 1, NC - 2 + c) + 1)
                else:
                    sp.wait_ge(num_ready, g * NB + HALF * (H - 3))
                row = (g * NC + c) * P
                cols = slice(H % 2 * HALF * GR, (H % 2 + 1) * HALF * GR)
                sp.dma_start(adj[:, c % 2, H % 2 * HALF:(H % 2 + 1) * HALF, :].rearrange("p b n -> p (b n)"),
                             adj_t[row:row + P, cols]).then_inc(half_loaded[H % 4], 16)
                if not computed(g, HALF * H):
                    exp_slot_free(sp, g, H)
                    for a in range(2):
                        sp.wait_ge(exp_sent[(2 * g + a) % 4], 32 * sent_no(c, 2 * g + a))
                    rows = sent_rows(c, g) + H % 2 * P
                    sp.dma_start(expo[:, H % 4, :], sent[rows:rows + P, :]).then_inc(exp_back[H % 4], 16)

            sp.wait_ge(x_loaded[0], 16)
            load_x(1)
            load(0, 0, 0, first=True)
            load_x(2)
            load_x(3)
            load(0, 0, 1, first=True)
            for q in range(4, NG):
                load_x(q)
            for p in range(6):
                if p == ATT:
                    for g in range(NG):
                        for H in range(NH):
                            before = (g, H - 4) if H >= 4 else (g - 1, H - 4 + NH)
                            if before[0] >= 0 and is_sent(*before):
                                send(*before)
                            att_half(g, H)
                else:
                    group(p, 0, first=p == 0)
                    with sp.Fori(1, NG) as g:
                        group(p, g)
            for b in range(GB):
                sp.wait_ge(x_ready, at(RES, 5, NG - 1, 1, b + 1))
                row = (NG - 1) * GR + b * P
                sp.dma_start(out[row:row + P, :], xres[:, (NG - 1) * GB + b, :]).then_inc(stored, 16)
            sp.wait_ge(stored, 16 * (NG - 1 + GB))

        @block.gpsimd
        def _(pool):
            nc.gpsimd.memset(ident[:, :], 0.0).then_inc(ident_zero, 1)
            nc.gpsimd.memset(neghalf[:, :], -0.5).then_inc(const_ready, 1)
            nc.gpsimd.memset(ident32[:, :], 0.0).then_inc(ident_zero, 1)
            pool.wait_ge(ident_zero, 2)
            nc.gpsimd.affine_select(out=ident32[:, :], in_=ident32[:, :], compare_op=ALU.not_equal, fill=1.0,
                                    base=0, pattern=[[-1, P]], channel_multiplier=1).then_inc(const_ready, 1)
            nc.gpsimd.affine_select(out=ident[:, :], in_=ident[:, :], compare_op=ALU.not_equal, fill=1.0,
                                    base=0, pattern=[[-1, P]], channel_multiplier=1).then_inc(const_ready, 1)
            pool.wait_ge(const_ready, 3)

            def rstd_of(p, g, u=0):
                pool.wait_ge(var_ready, at(NORM, p, g, 2, 2))
                nc.gpsimd.tensor_tensor(out=rstd[:, u, :], in0=vare[:, u, :], in1=neghalf[:, 0:GB], op=ALU.pow)\
                    .then_inc(rstd_ready, 1)
                pool.wait_ge(rstd_ready, at(NORM, p, g))
                nc.gpsimd.tensor_tensor(out=shift[:, u, :], in0=nmean[:, u, :], in1=rstd[:, u, :], op=ALU.mult)\
                    .then_inc(shift_ready, 1)

            def tail(p, g):
                if p in SELF:
                    pool.wait_ge(mov_ready, at(MOVE, p - 1, g, GB, GB))
                    if not (isinstance(g, int) and p == 0):
                        pool.wait_ge(sum_ready, at(SELF, p, g, 1, 0))
                    rows = mov[p % 2][:, bass.ds(g * GB, GB), :]
                    nc.gpsimd.tensor_tensor(out=own[:, :, :], in0=rows[:, :, 0:F], in1=rows[:, :, LO:LO + F], op=ALU.add)\
                        .then_inc(own_ready, 1)
                if p == 0:
                    pool.wait_ge(row_ready, at([0], p, g, 2, 2))
                    nc.gpsimd.tensor_tensor(out=rowp[:, :], in0=rowc[:, :], in1=neghalf[:, 0:GB], op=ALU.pow)\
                        .then_inc(rowp_ready, 1)
                if p in NORM:
                    rstd_of(p, g)
                if p == 1:
                    for r in range(2):
                        pool.wait_ge(ssqc_ready, at([1], p, g, 2, r + 1))
                        nc.gpsimd.tensor_tensor(out=rnorm[:, 2 * r:2 * r + 2], in0=ssqc[:, 2 * r:2 * r + 2],
                                                in1=neghalf[:, 0:2], op=ALU.pow).then_inc(rnorm_ready, 1)

            with pool.Fori(0, NG, 2) as g:
                rstd_of(PRE, g, 0)
                rstd_of(PRE, g + 1, 1)
            pool.wait_ge(diag_one, 1)
            nc.gpsimd.tensor_tensor(out=d[:, :], in0=diag[:, :], in1=neghalf[:, :], op=ALU.pow).then_inc(d_ready, 1)
            for p in [0, 1, 2, 3]:
                if p == 0:
                    tail(0, 0)
                    with pool.Fori(1, NG) as g:
                        tail(p, g)
                else:
                    with pool.Fori(0, NG) as g:
                        tail(p, g)

        @block.tensor
        def _(pe):
            def product(p, g, c, b, k, first, last):
                jb = GB * c + k
                m = mov[p % 2]
                cols = slice(b * P, (b + 1) * P)
                hi, lo = ahi[:, c % 2, k, cols], alo[:, c % 2, k, cols]
                if p in CROSS:
                    both = m[:, jb, :].rearrange("p (s n) -> p s n", s=2)[:, :, 0:F]
                    nc.tensor.matmul(acc[:, b, :].rearrange("p (s n) -> p s n", s=2), hi, both, start=first, stop=False)
                    return nc.tensor.matmul(acc[:, b, 0:F], lo, m[:, jb, 0:F], start=False, stop=last)
                n = F + 1
                nc.tensor.matmul(acc[:, b, 0:n], hi, m[:, jb, 0:n], start=first, stop=False)
                nc.tensor.matmul(acc[:, b, 0:F], hi, m[:, jb, LO:LO + F], start=False, stop=False)
                return nc.tensor.matmul(acc[:, b, 0:n], lo, m[:, jb, 0:n], start=False, stop=last)

            def product_turned(g, c, f, k, first, last):
                m = mov[TURNED % 2][:, GB * c + k, :]
                hi, lo = m[:, f * P:(f + 1) * P], m[:, LO + f * P:LO + (f + 1) * P]
                nc.tensor.matmul(acc[:, f, :], hi, ahi[:, c % 2, k, :], start=first, stop=False)
                nc.tensor.matmul(acc[:, f, :], hi, alo[:, c % 2, k, :], start=False, stop=False)
                return nc.tensor.matmul(acc[:, f, :], lo, ahi[:, c % 2, k, :], start=False, stop=last)

            def turned_group(g, tp, tg):
                for c in range(NC):
                    pe.wait_ge(split_ready, chunk_no(TURNED, g, c) + 1)
                    moving_there(TURNED, g, c)
                    for b in range(GB):
                        f = b // (GB // FB)
                        half = range(b % (GB // FB) * FB, b % (GB // FB) * FB + FB)
                        if c == 0 and half[0] == 0:
                            if isinstance(g, int) and g == 0:
                                pe.wait_ge(ev_ready, at(ALL, TURNED - 1, NG - 1, GB, f + 1))
                            else:
                                pe.wait_ge(ev_ready, at(ALL, TURNED, g - 1, GB, GB // FB * (f + 1)))
                        for k in half:
                            last = product_turned(g, c, f, k, c == 0 and k == 0, c == NC - 1 and k == GB - 1)
                        if c == NC - 1 and half[-1] == GB - 1:
                            last.then_inc(acc_ready, GB // FB)
                        elif c < NC - 1 and b == GB - 1:
                            last.then_inc(chunk_done, 1)
                        if (c, b) in PLACES:
                            step(PLACES[c, b], tp, tg)

            def bank_free(p, g, b):
                if isinstance(g, int) and g == 0:
                    if p == TURNED + 1:
                        pe.wait_ge(ev_ready, at(ALL, TURNED, NG - 1, GB, min(GB // FB * (b + 1), GB)))
                    elif p > 0:
                        pe.wait_ge(ev_ready, at(ALL, p - 1, NG - 1, GB, b + 1))
                else:
                    pe.wait_ge(ev_ready, at(ALL, p, g - 1, GB, b + 1))

            def turn(p, g, r):
                pe.wait_ge(h_ready, at(SMALL, p, g))
                if p == PRE:
                    if g > 0:
                        pe.wait_ge(hT_ready, at(SMALL, p, g - 1, 2, r + 1))
                elif r == 1:
                    pe.wait_ge(hT_ready, at(SMALL, p, g, 2, 1))
                elif not isinstance(g, int) or g > 0:
                    pe.wait_ge(hT_ready, at(SMALL, p, g - 1, 2, 2))
                    if p == 1:
                        pe.wait_ge(gnT_ready, at([1], p, g - 1, 2, 2))
                else:
                    before = SMALL[SMALL.index(p) - 1]
                    pe.wait_ge(hT_ready, at(SMALL, before, NG - 1, 2, 2))
                    if p == 2:
                        pe.wait_ge(gnT_ready, at([1], 1, NG - 1, 2, 2))
                transposes(r, work(p, g)[1], psT2 if p == PRE and r == 1 else psT).then_inc(h_turned, 1)

            def transposes(r, hsp, to):
                for q in range(2 * FB):
                    for b in range(2):
                        last = nc.tensor.transpose(to[:, q, b * P:(b + 1) * P],
                                                   hsp[:, q // FB, 2 * r + b, (q % FB) * P:(q % FB + 1) * P],
                                                   ident[:, :])
                return last

            def small(p, g, r):
                whi, wlo = weights_of[p]
                if p == TURNED:
                    pe.wait_ge(h_ready, at(SMALL, p, g))
                else:
                    pe.wait_ge(hT_ready, at(SMALL, p, g, 2, r + 1))
                if p == PRE:
                    if g > 0:
                        pe.wait_ge(mov_ready, at(MOVE, p, g - 1, GB, 2 * r + 2))
                elif r == 1:
                    pe.wait_ge(mov_ready, at(MOVE, p, g, GB, 2))
                    if p == 1:
                        pe.wait_ge(gn_ready, at([1], p, g, GB, 2))
                elif not isinstance(g, int) or g > 0:
                    pe.wait_ge(mov_ready, at(MOVE, p, g - 1, GB, 4))
                    if p == 1:
                        pe.wait_ge(gn_ready, at([1], p, g - 1, GB, 4))
                elif p > PRE:
                    pe.wait_ge(mov_ready, at(MOVE, p - 1, NG - 1, GB, 4))
                    if p == 2:
                        pe.wait_ge(gn_ready, at([1], 1, NG - 1, GB, 4))
                if p == 3:
                    both = slice(2 * r * P, 2 * (r + 1) * P)
                    for h in range(FB):
                        to, wc = psW[:, h * F:(h + 1) * F], slice(h * P, (h + 1) * P)
                        for f in range(FB):
                            nc.tensor.matmul(to, whi[:, f, wc], hT[:, f, both], start=f == 0, stop=False)
                            nc.tensor.matmul(to, whi[:, f, wc], hT[:, FB + f, both], start=False, stop=False)
                            nc.tensor.matmul(to, wlo[:, f, wc], hT[:, f, both], start=False, stop=f == FB - 1)
                    whi, wlo = whi[:, :, F:2 * F], wlo[:, :, F:2 * F]
                for b in range(2):
                    rows = slice((2 * r + b) * P, (2 * r + b + 1) * P)
                    to = small_bank(p, 2 * r + b)
                    for f in range(FB):
                        nc.tensor.matmul(to, hT[:, f, rows], whi[:, f, :], start=f == 0, stop=False)
                        nc.tensor.matmul(to, hT[:, f, rows], wlo[:, f, :], start=False, stop=False)
                        last = nc.tensor.matmul(to, hT[:, FB + f, rows], whi[:, f, :], start=False,
                                                stop=f == FB - 1)
                last.then_inc(small_ready, 1)

            def turn_gn(p, g, r):
                pe.wait_ge(gn_ready, at([1], p, g, GB, 2 * r + 2))
                if r == 0:
                    pe.wait_ge(hT_ready, at(SMALL, p, g, 2, 2))
                else:
                    pe.wait_ge(gnT_ready, at([1], p, g, 2, 1))
                transposes(r, hsp, psT).then_inc(gn_turned, 1)

            def step(name, p, g):
                if name == "T0":
                    if p != TURNED:
                        turn(p, g, 0)
                elif name == "W0T1":
                    small(p, g, 0)
                    if p != TURNED:
                        turn(p, g, 1)
                elif name == "W1":
                    small(p, g, 1)
                elif name == "T0T1":
                    turn(p, g, 0)
                    turn(p, g, 1)
                elif name == "W0":
                    small(p, g, 0)
                elif p == 1:
                    turn_gn(p, g, int(name[1]))

            PLACES = {(3, 3): "T0", (4, 0): "W0T1", (5, 0): "W1", (6, 0): "G0", (6, 2): "G1"}
            START_PLACES = {(0, 0): [("W0", 1)], (0, 1): [("W1", 1)], (0, 2): [("T0T1", 2)], (0, 3): [("W0", 2)],
                            (1, 0): [("W1", 2), ("T0T1", 3)], (1, 1): [("W0", 3)], (1, 2): [("W1", 3)]}
            for q in range(4, NC):
                for i, name in enumerate(["T0T1", "W0", "W1"]):
                    START_PLACES[q - 2, i] = [(name, q)]
            ATT_PLACES = [{10: "T0", 12: "W0T1", 15: "W1", 18: "G0", 20: "G1"}, {19: "T0", 22: "W0T1", 26: "W1"}]

            def moving_there(p, g, c):
                if isinstance(g, int) and g == 0:
                    pe.wait_ge(mov_ready, at(MOVE, p - 1, c, GB, 4))

            def group(p, g, tp, tg):
                for c in range(NC):
                    pe.wait_ge(split_ready, chunk_no(p, g, c) + 1)
                    moving_there(p, g, c)
                    for b in range(GB):
                        if c == 0:
                            bank_free(p, g, b)
                        for k in range(GB):
                            last = product(p, g, c, b, k, c == 0 and k == 0, c == NC - 1 and k == GB - 1)
                        if c == NC - 1:
                            last.then_inc(acc_ready, 1)
                        elif b == GB - 1:
                            last.then_inc(chunk_done, 1)
                        if tp in SMALL and tp != PRE and (c, b) in PLACES:
                            step(PLACES[c, b], tp, tg)
                        if tp == PRE:
                            for name, q in START_PLACES.get((c, b), []):
                                step(name, PRE, q)

            def similarity(g, j):
                n = g * NB + j
                before = (g, j - 2) if j >= 2 else (g - 1, j - 2 + NB)
                if before[0] >= 0:
                    if not turned(*before):
                        pe.wait_ge(exp_ready, exp_no(*before))
                    else:
                        pe.wait_ge(num_ready, n - 1)
                if computed(g, j):
                    last = cosines(g, j)
                    k = turned(g, j)
                    if k > 0:
                        pe.wait_ge(exp_ready, exp_no(g, j - 1))
                    for b in range(k):
                        last = nc.tensor.transpose(psS[:, j % 2, b * P:(b + 1) * P],
                                                   exp_of(GB * g + b)[:, k * P:(k + 1) * P], ident32[:, :])
                    last.then_inc(sim_ready, 1)
                    return
                H = j // HALF
                pe.wait_ge(exp_back[H % 4], 16 * back_no(g, H))
                half = expo[:, H % 4, :].rearrange("p (b n) -> p b n", b=GB)
                for b in range(GB):
                    last = nc.tensor.transpose(psS[:, j % 2, b * P:(b + 1) * P],
                                               half[:, b, (j % HALF) * P:(j % HALF + 1) * P], ident32[:, :])
                last.then_inc(sim_ready, 1)

            def cosines(g, j):
                if g == 0 and j % GB == 0:
                    pe.wait_ge(gnT_ready, at([1], 1, j // GB, 2, 2))
                k = turned(g, j)
                rows = slice(g * GR + k * P, (g + 1) * GR)
                for f in range(FB):
                    hi, lo = gnT[:, f, j * P:(j + 1) * P], gnT[:, FB + f, j * P:(j + 1) * P]
                    mhi, mlo = gnT[:, f, rows], gnT[:, FB + f, rows]
                    nc.tensor.matmul(psS[:, j % 2, k * P:], hi, mhi, start=f == 0, stop=False)
                    nc.tensor.matmul(psS[:, j % 2, k * P:], hi, mlo, start=False, stop=False)
                    last = nc.tensor.matmul(psS[:, j % 2, k * P:], lo, mhi, start=False, stop=f == FB - 1)
                return last

            def att_group(g, tp, tg):
                for j in range(NB):
                    if j + LEAD < NB:
                        similarity(g, j + LEAD)
                    elif g < NG - 1:
                        similarity(g + 1, j + LEAD - NB)
                    pe.wait_ge(num_split, g * NB + j + 1)
                    if j % GB == 0:
                        moving_there(ATT, g, j // GB)
                    for b in range(GB):
                        if j == 0:
                            bank_free(ATT, g, b)
                        last = product(ATT, g, j // GB, b, j % GB, j == 0, j == NB - 1)
                        if j == NB - 1:
                            last.then_inc(acc_ready, 1)
                        elif b == GB - 1:
                            last.then_inc(block_done, 1)
                    if j in ATT_PLACES[g > 0]:
                        step(ATT_PLACES[g > 0][j], tp, tg)

            def keep_warm(n):
                for _ in range(n):
                    nc.tensor.matmul(acc[:, GB - 1, 0:P], ident[:, :], ident[:, :], start=True, stop=True)

            pe.wait_ge(const_ready, 3)
            pe.wait_ge(var_ready, 2)
            keep_warm(WARM[0])
            pe.wait_ge(w_ready, 1)
            pe.wait_ge(ones_ready, 2)
            for s in ["T0T1", "W0", "W1"]:
                step(s, PRE, 0)
            keep_warm(WARM[1])
            step("T0T1", PRE, 1)
            for p in range(6):
                if p == 1:
                    pe.wait_ge(w_ready, 2)
                if p == ATT:
                    for j in range(LEAD):
                        similarity(0, j)
                    for g in range(NG):
                        att_group(g, *((ATT, g - 1) if g else (1, NG - 1)))
                elif p == TURNED:
                    turned_group(0, p - 1, NG - 1)
                    with pe.Fori(1, NG) as g:
                        turned_group(g, p, g - 1)
                else:
                    group(p, 0, p - 1, NG - 1)
                    with pe.Fori(1, NG) as g:
                        group(p, g, p, g - 1)

        @block.scalar
        def _(act):
            act.dma_start(xres[:, 0:GB, :].rearrange("p b n -> p (b n)"), x[0:P, :]).then_inc(x_loaded[0], 16)
            act.dma_start(wraw[0], w0).then_inc(w0_loaded, 16)

            def hi_of_weights(part, loaded, count):
                act.wait_ge(loaded, count)
                nc.scalar.activation(wsp[:, 0, part], shared[:, part], ACT.Copy, scale=W_SCALE).then_inc(w_hi, 1)

            def split(p, g, c):
                act.wait_ge(adj_loaded[c % 2], at(PLAIN, p, g, 16 * NC // 2, (c // 2 + 1) * 16))
                first = isinstance(g, int) and g == 0
                if c >= 2:
                    act.wait_ge(chunk_done, at(PLAIN, p, g, NC - 1, c - 1))
                elif not (first and p == 0):
                    if c == 1:
                        act.wait_ge(acc_ready, at(ALL, p, g, GB, 0))
                    elif first and p == ATT + 1:
                        act.wait_ge(block_done, (NB - 1) * (NG - 1) + NB - GB)
                    else:
                        act.wait_ge(chunk_done, at(PLAIN, p, g, NC - 1, 0))
                nc.scalar.activation(ahi[:, c % 2, :, :], adj[:, c % 2, :, :], ACT.Copy, scale=ADJ_SCALE)\
                    .then_inc(split_hi, 1)

            def ev_used(p, g):
                if p == 0:
                    act.wait_ge(sum_ready, at(SELF, p, g))
                    act.wait_ge(row_ready, at([0], p, g, 2, 2))
                else:
                    act.wait_ge(scaled, at(SCALED, p, g, GB, GB))

            def o_used(p, g):
                if p == 0:
                    act.wait_ge(mov_ready, at(MOVE, p, g, GB, GB))
                elif p == 5:
                    act.wait_ge(x_ready, at(RES, p, g))
                else:
                    act.wait_ge(h_ready, at(SMALL, p, g))

            def evacuate(p, g):
                if p == TURNED:
                    return
                first = isinstance(g, int) and g == 0
                if p in CROSS:
                    o_used(*((p - 1, NG - 1) if first else (p, g - 1)))
                elif not first:
                    ev_used(p, g - 1)
                elif p == ATT:
                    ev_used(0, NG - 1)
                for b in range(GB):
                    act.wait_ge(acc_ready, at(ALL, p, g, GB, b + 1))
                    if p in CROSS:
                        nc.scalar.activation(o[:, b, :], acc[:, b, F:2 * F], ACT.Copy, scale=1.0 / ADJ_SCALE)\
                            .then_inc(cross_ready, 1)
                    else:
                        nc.scalar.activation(ev[:, b, :], acc[:, b, 0:F + 1], ACT.Copy,
                                             scale=1.0 if p == ATT else 1.0 / ADJ_SCALE).then_inc(ev_ready, 1)

            def blocks(g, b, n=1):
                return bass.ds(g * GB + b, n)

            def hi_of_t(p, g):
                act.wait_ge(sum_ready, at(SELF, p, g))
                act.wait_ge(d_ready, 1)
                for b in range(GB):
                    nc.scalar.activation(mov[1][:, blocks(g, b), 0:F], o[:, b, :], ACT.Copy, scale=d[:, blocks(g, b)])\
                        .then_inc(mov_hi, 1)

            def hi_of_h(p, g):
                o, hsp, u = work(p, g)
                if p == TURNED:
                    act.wait_ge(ev_ready, at(ALL, p, g, GB, GB))
                    q, e = (p - 1, NG - 1) if isinstance(g, int) and g == 0 else (p, g - 1)
                    act.wait_ge(small_ready, at(SMALL, q, e, 2, 2))
                    nc.scalar.activation(hT[:, 0:FB, :], oT, ACT.Relu).then_inc(h_hi, GB)
                    return
                act.wait_ge(shift_ready, at(NORM, p, g))
                if p == PRE:
                    if g >= 2:
                        act.wait_ge(h_turned, at(SMALL, p, g - 2, 2, 2))
                elif not isinstance(g, int) or g > 0:
                    act.wait_ge(h_turned, at(SMALL, p, g - 1, 2, 2))
                    if p == 1:
                        act.wait_ge(gn_turned, at([1], p, g - 1, 2, 2))
                else:
                    act.wait_ge(h_turned, at(SMALL, SMALL[SMALL.index(p) - 1], NG - 1, 2, 2))
                    if p == 2:
                        act.wait_ge(gn_turned, at([1], 1, NG - 1, 2, 2))
                for b in range(GB):
                    nc.scalar.activation(hsp[:, 0, b, :], xres[:, blocks(g, b), :].rearrange("p a n -> p (a n)"),
                                         ACT.Relu, bias=shift[:, u, b:b + 1], scale=rstd[:, u, b:b + 1])\
                        .then_inc(h_hi, 1)

            def keep_hT(p, g, r):
                act.wait_ge(h_turned, at(SMALL, p, g, 2, r + 1))
                if not isinstance(g, int) or g > 0:
                    act.wait_ge(small_ready, at(SMALL, p, g - 1, 2, r + 1))
                elif p > PRE:
                    act.wait_ge(small_ready, at(SMALL, SMALL[SMALL.index(p) - 1], NG - 1, 2, r + 1))
                nc.scalar.activation(hT[:, :, 2 * P * r:2 * P * (r + 1)],
                                     (psT2 if p == PRE and r == 1 else psT)[:, :, :], ACT.Copy)\
                    .then_inc(hT_ready, 1)

            def small_out(p, b):
                return small_bank(p, b)[:, -F:]

            def hi_of_small(p, g, r):
                act.wait_ge(small_ready, at(SMALL, p, g, 2, r + 1))
                if p == 3:
                    nc.scalar.activation(directT[:, bass.ds(g * FB, FB), 2 * P * r:2 * P * (r + 1)],
                                         psW[:, :].rearrange("p (f n) -> p f n", f=FB), ACT.Copy, scale=1.0 / W_SCALE)\
                        .then_inc(direct_ready, 2)
                for b in (2 * r, 2 * r + 1):
                    if p == TURNED:
                        nc.scalar.activation(direct[:, blocks(g, b), :], small_bank(p, b)[:, 0:F], ACT.Copy, scale=1.0 / W_SCALE)\
                            .then_inc(direct_ready, 1)
                    if p == 1:
                        nc.scalar.activation(junk[:, b, :], small_out(p, b), ACT.Square, scale=1.0 / W_SCALE,
                                             accum_out=ssq[:, b:b + 1]).then_inc(ssq_ready, 1)
                    nc.scalar.activation(mov[(p + 1) % 2][:, blocks(g, b), 0:F], small_out(p, b), ACT.Copy,
                                         scale=dinv_w[:, blocks(g, b)] if p == 2 else 1.0 / W_SCALE)\
                        .then_inc(mov_hi, 1)

            def hi_of_gn(p, g, r):
                act.wait_ge(rnorm_ready, at([1], p, g, 2, r + 1))
                act.wait_ge(mov_ready, at(MOVE, p, g, GB, 2 * r + 2))
                act.wait_ge(h_turned, at(SMALL, p, g, 2, r + 1))
                for b in (2 * r, 2 * r + 1):
                    nc.scalar.activation(hsp[:, 0, b, :], small_out(p, b), ACT.Copy, scale=rnorm[:, b:b + 1])\
                        .then_inc(gn_hi, 1)

            def keep_gnT(p, g, r):
                act.wait_ge(gn_turned, at([1], p, g, 2, r + 1))
                nc.scalar.activation(gnT[:, :, bass.ds(g * GR + 2 * P * r, 2 * P)], psT[:, :, :], ACT.Copy)\
                    .then_inc(gnT_ready, 1)

            def stage(name, p, g):
                if name == "ev":
                    evacuate(p, g)
                elif name == "h":
                    if p == 0:
                        hi_of_t(p, g)
                    elif p in SMALL:
                        hi_of_h(p, g)
                elif p in SMALL and name == "T0":
                    if p != TURNED:
                        keep_hT(p, g, 0)
                elif p in SMALL and name == "W0":
                    hi_of_small(p, g, 0)
                elif p in SMALL and name == "T1":
                    if p != TURNED:
                        keep_hT(p, g, 1)
                elif p in SMALL and name == "W1":
                    hi_of_small(p, g, 1)
                elif p == 1 and name in ("n0", "n1"):
                    hi_of_gn(p, g, int(name[1]))
                elif p == 1 and name in ("g0", "g1"):
                    keep_gnT(p, g, int(name[1]))

            PLACES = {0: ["ev"], 3: ["h"], 4: ["T0"], 5: ["W0", "T1", "n0"], 6: ["W1", "n1"], 7: ["g0", "g1"]}
            ATT_PLACES = [{2: ["ev"], 10: ["h"], 14: ["T0"], 16: ["W0", "T1"], 17: ["n0"], 19: ["W1"],
                           20: ["n1"], 22: ["g0"], 24: ["g1"]},
                          {2: ["ev"], 17: ["h"], 23: ["T0"], 26: ["W0", "T1"], 30: ["W1"]}]

            def group(p, g, tp, tg):
                for c in range(NC):
                    split(p, g, c)
                    for name in PLACES.get(c, []):
                        stage(name, tp, tg)

            def exponential(g, j):
                H = j // HALF
                if j % HALF == 0:
                    exp_slot_free(act, g, H)
                act.wait_ge(sim_ready, g * NB + j + 1)
                first = turned(g, j) * P
                nc.scalar.activation(exp_of(j)[:, first:], psS[:, j % 2, first:], ACT.Exp,
                                     scale=1.0 / (GN_SCALE * GN_SCALE)).then_inc(exp_ready, 1)

            def hi_of_numerators(g, j):
                n = g * NB + j
                act.wait_ge(num_ready, n + 1)
                if n == 0:
                    act.wait_ge(chunk_done, 2 * NG * (NC - 1))
                elif n == GB:
                    act.wait_ge(acc_ready, 2 * NG * GB)
                elif n >= 2 * GB:
                    if (n - 2 * GB) % NB == NB - 1:
                        act.wait_ge(acc_ready, at(ALL, ATT, g, GB, 0))
                    else:
                        before = n - 2 * GB
                        act.wait_ge(block_done, before // NB * (NB - 1) + before % NB + 1)
                nc.scalar.activation(ahi[:, (j // GB) % 2, j % GB, :], nums[:, n % NUMS, :], ACT.Copy, scale=P_SCALE)\
                    .then_inc(num_hi, 1)

            def att_group(g, tp, tg):
                for j in range(NB):
                    if computed(g, j):
                        exponential(g, j)
                    if j > 0:
                        hi_of_numerators(g, j - 1)
                    elif g > 0:
                        hi_of_numerators(g - 1, NB - 1)
                    for name in ATT_PLACES[g > 0].get(j, []):
                        stage(name, tp, tg)

            stage("h", PRE, 0)
            hi_of_weights(slice(0, wofs[1]), w0_loaded, 16)
            split(0, 0, 0)
            for q in range(NG):
                for name in ["T0", "T1", "W0"]:
                    stage(name, PRE, q)
                if q + 1 < NG:
                    stage("h", PRE, q + 1)
                stage("W1", PRE, q)
                if q != 1:
                    split(0, 0, max(1, q))
            hi_of_weights(slice(wofs[1], wofs[5]), w_loaded, 16 * 4)
            for p in range(6):
                if p == ATT:
                    act.wait_ge(dinv_ready, 2 * NG)
                    for g in range(NG):
                        att_group(g, *((ATT, g - 1) if g else (1, NG - 1)))
                    hi_of_numerators(NG - 1, NB - 1)
                else:
                    if p > 0:
                        group(p, 0, p - 1, NG - 1)
                    with act.Fori(1, NG) as g:
                        group(p, g, p, g - 1)
            stage("ev", 5, NG - 1)

        @block.vector
        def _(dve):
            for i in range(2):
                nc.vector.memset(mov[i][:, :, F:LO], 1.0).then_inc(ones_ready, 1)

            def blocks(g, b, n=1):
                return bass.ds(g * GB + b, n)

            def split(p, g, c):
                dve.wait_ge(split_hi, chunk_no(p, g, c) + 1)
                nc.vector.scalar_tensor_tensor(alo[:, c % 2, :, :].rearrange("p b n -> p (b n)"),
                                               adj[:, c % 2, :, :].rearrange("p b n -> p (b n)"), ADJ_SCALE,
                                               ahi[:, c % 2, :, :].rearrange("p b n -> p (b n)"),
                                               ALU.mult, ALU.subtract).then_inc(split_ready, 1)

            def add_cross(p, g, b):
                dve.wait_ge(cross_ready, at(CROSS, p, g, GB, b + 1))
                nc.vector.scalar_tensor_tensor(o[:, b, :], acc[:, b, 0:F], 1.0 / ADJ_SCALE, o[:, b, :],
                                               ALU.mult, ALU.add).then_inc(ev_ready, 1)

            def add_direct(g):
                before = (TURNED - 1, NG - 1) if isinstance(g, int) and g == 0 else (TURNED, g - 1)
                dve.wait_ge(h_ready, at(SMALL, *before))
                dve.wait_ge(direct_ready, at(DIRECT, TURNED - 1, g, GB, GB))
                for f in range(FB):
                    dve.wait_ge(acc_ready, at(ALL, TURNED, g, GB, GB // FB * (f + 1)))
                    nc.vector.scalar_tensor_tensor(oT[:, f, :], acc[:, f, :], 1.0 / ADJ_SCALE,
                                                   directT[:, bass.ds(g * FB + f, 1), :].rearrange("p a n -> p (a n)"),
                                                   ALU.mult, ALU.add).then_inc(ev_ready, GB // FB)

            def epilogue(p, g):
                if p == TURNED:
                    return
                dve.wait_ge(ev_ready, at(ALL, p, g, GB, GB))
                if p in SELF:
                    dve.wait_ge(own_ready, at(SELF, p, g))
                    nc.vector.tensor_tensor(o[:, :, :], ev[:, :, 0:F] if p == 0 else o[:, :, :], own[:, :, :], ALU.add)\
                        .then_inc(sum_ready, 1)
                    if p == 0:
                        nc.vector.tensor_scalar(rowm[:, :], ev[:, :, F], 0.0, None, ALU.is_gt)\
                            .then_inc(row_ready, 1)
                        nc.vector.tensor_scalar(rowc[:, :], ev[:, :, F], TINY, None, ALU.max).then_inc(row_ready, 1)
                    dve.wait_ge(sum_ready, at(SELF, p, g))
                if p == 0:
                    return
                if p == 1:
                    for b in range(GB):
                        nc.vector.tensor_scalar(o[:, b, :], o[:, b, :], d[:, blocks(g, b)], None, ALU.mult)\
                            .then_inc(scaled, 1)
                elif p == 2:
                    nc.vector.reciprocal(rden[:, :], ev[:, :, F]).then_inc(den_ready, 1)
                    dve.wait_ge(den_ready, at([2], p, g))
                    for b in range(GB):
                        nc.vector.scalar_tensor_tensor(o[:, b, :], ev[:, b, 0:F], rden[:, b:b + 1], bg[:, :],
                                                       ALU.mult, ALU.add).then_inc(scaled, 1)
                elif p == 3:
                    for b in range(GB):
                        nc.vector.scalar_tensor_tensor(o[:, b, :], o[:, b, :], dinv[:, blocks(g, b)], b2[:, :],
                                                       ALU.mult, ALU.add).then_inc(scaled, 1)
                else:
                    dve.wait_ge(direct_ready, at(DIRECT, p - 1, g, GB, GB))
                    nc.vector.tensor_tensor(o[:, :, :], o[:, :, :], direct[:, blocks(g, 0, GB), :], ALU.add)\
                        .then_inc(preact, 1)

            def residual(p, g):
                rows = xres[:, blocks(g, 0, GB), :]
                if p in SCALED:
                    dve.wait_ge(scaled, at(SCALED, p, g, GB, GB))
                elif p == 5:
                    dve.wait_ge(preact, at([5], p, g))
                if p == 2:
                    nc.vector.tensor_tensor(rows, o[:, :, :], rows, ALU.add).then_inc(x_ready, 1)
                elif p in RES:
                    nc.vector.scalar_tensor_tensor(rows, o[:, :, :], 0.0, rows, ALU.max, ALU.add).then_inc(x_ready, 1)

            def norm_stats(p, g):
                if p == PRE:
                    dve.wait_ge(x_loaded[g], 16)
                else:
                    dve.wait_ge(x_ready, at(RES, p, g))
                dve.sem_inc(passed, 1)
                u = work(p, g)[2]
                for b in range(GB):
                    nc.vector.bn_stats(stats[:, b, :], xres[:, blocks(g, b), :].rearrange("p a n -> p (a n)"))\
                        .then_inc(stats_ready, 1)
                dve.wait_ge(stats_ready, at(NORM, p, g, GB, GB))
                dve.sem_inc(passed, 1)
                for b in range(GB):
                    nc.vector.bn_aggr(mv[:, u, b, :], stats[:, b, :]).then_inc(mv_ready, 1)
                dve.wait_ge(mv_ready, at(NORM, p, g, GB, GB))
                nc.vector.tensor_scalar(nmean[:, u, :], mv[:, u, :, 0], -1.0, None, ALU.mult).then_inc(var_ready, 1)
                nc.vector.tensor_scalar(vare[:, u, :], mv[:, u, :, 1], LN_EPS, None, ALU.add).then_inc(var_ready, 1)

            def normalise(p, g):
                o, _, u = work(p, g)
                dve.wait_ge(rstd_ready, at(NORM, p, g))
                for b in range(GB):
                    nc.vector.tensor_scalar(o[:, b, :], xres[:, blocks(g, b), :].rearrange("p a n -> p (a n)"),
                                            mv[:, u, b, 0:1], rstd[:, u, b:b + 1], ALU.subtract, ALU.mult)\
                        .then_inc(normed, 1)

            def lo_of_h(p, g):
                o, hsp, _ = work(p, g)
                if p in NORM:
                    dve.wait_ge(normed, at(NORM, p, g, GB, GB))
                dve.wait_ge(h_hi, at(SMALL, p, g, GB, GB))
                if p == TURNED:
                    nc.vector.scalar_tensor_tensor(hT[:, FB:2 * FB, :], oT, 0.0, hT[:, 0:FB, :],
                                                   ALU.max, ALU.subtract).then_inc(h_ready, 1)
                    return
                nc.vector.scalar_tensor_tensor(hsp[:, 1, :, :], o[:, :, :], 0.0, hsp[:, 0, :, :],
                                               ALU.max, ALU.subtract).then_inc(h_ready, 1)

            def lo_of_t(p, g):
                for b in range(GB):
                    dve.wait_ge(mov_hi, at(MOVE, p, g, GB, b + 1))
                    nc.vector.scalar_tensor_tensor(mov[1][:, blocks(g, b), LO:LO + F], o[:, b, :], d[:, blocks(g, b)],
                                                   mov[1][:, blocks(g, b), 0:F], ALU.mult, ALU.subtract)\
                        .then_inc(mov_ready, 1)
                dve.wait_ge(rowp_ready, at([0], p, g))
                nc.vector.tensor_tensor(dinv[:, blocks(g, 0, GB)], rowp[:, :], rowm[:, :], ALU.mult)\
                    .then_inc(dinv_ready, 1)
                nc.vector.scalar_tensor_tensor(dinv_w[:, blocks(g, 0, GB)], rowp[:, :], 1.0 / W_SCALE, rowm[:, :],
                                               ALU.mult, ALU.mult).then_inc(dinv_ready, 1)

            def small_out(p, b):
                return small_bank(p, b)[:, -F:]

            def lo_of_small(p, g, r):
                for b in (2 * r, 2 * r + 1):
                    dve.wait_ge(mov_hi, at(MOVE, p, g, GB, b + 1 if p == TURNED else 2 * r + 2))
                    m = mov[(p + 1) % 2]
                    nc.vector.scalar_tensor_tensor(m[:, blocks(g, b), LO:LO + F], small_out(p, b),
                                                   dinv_w[:, blocks(g, b)] if p == 2 else 1.0 / W_SCALE,
                                                   m[:, blocks(g, b), 0:F], ALU.mult, ALU.subtract)\
                        .then_inc(mov_ready, 1)

            def guard_norm(p, g, r):
                dve.wait_ge(ssq_ready, at([1], p, g, GB, 2 * r + 2))
                nc.vector.tensor_scalar(ssqc[:, 2 * r:2 * r + 2], ssq[:, 2 * r:2 * r + 2], NORM_EPS * NORM_EPS, None,
                                        ALU.max).then_inc(ssqc_ready, 1)

            def lo_of_gn(p, g, r):
                for b in (2 * r, 2 * r + 1):
                    dve.wait_ge(gn_hi, at([1], p, g, GB, 2 * r + 2))
                    nc.vector.scalar_tensor_tensor(hsp[:, 1, b, :], small_out(p, b), rnorm[:, b:b + 1],
                                                   hsp[:, 0, b, :], ALU.mult, ALU.subtract).then_inc(gn_ready, 1)

            def stage(name, p, g):
                if name == "ev" and p in CROSS:
                    for b in range(GB):
                        add_cross(p, g, b)
                elif name == "ev" and p == TURNED:
                    add_direct(g)
                elif name == "epi":
                    epilogue(p, g)
                elif name == "x" and p in RES:
                    residual(p, g)
                elif name == "norm" and p in NORM:
                    normalise(p, g)
                elif name == "stats" and p in NORM:
                    norm_stats(p, g)
                elif name == "h":
                    if p == 0:
                        lo_of_t(p, g)
                    elif p in SMALL:
                        lo_of_h(p, g)
                elif p in SMALL and name == "W0":
                    if p == 1:
                        guard_norm(p, g, 0)
                    lo_of_small(p, g, 0)
                elif p in SMALL and name == "W1":
                    if p == 1:
                        guard_norm(p, g, 1)
                    lo_of_small(p, g, 1)
                elif p == 1 and name in ("n0", "n1"):
                    lo_of_gn(p, g, int(name[1]))

            PLACES = {0: ["ev"], 1: ["epi"], 2: ["x", "stats"], 3: ["norm", "h"], 5: ["W0", "n0"], 6: ["W1", "n1"]}
            ATT_PLACES = [{2: ["ev"], 4: ["epi"], 6: ["x"], 7: ["stats"], 9: ["norm"], 10: ["h"], 16: ["W0"], 17: ["n0"],
                           19: ["W1"], 20: ["n1"]},
                          {4: ["epi"], 8: ["x"], 11: ["stats"], 14: ["norm"], 17: ["h"], 26: ["W0"], 30: ["W1"]}]

            def group(p, g, tp, tg):
                for c in range(NC):
                    split(p, g, c)
                    for name in PLACES.get(c, []):
                        stage(name, tp, tg)

            def numerators(g, j):
                n, H = g * NB + j, j // HALF
                if j % HALF == 0:
                    dve.wait_ge(half_loaded[H % 4], 16 * (g * NH // 4 + H // 4 + 1))
                if n >= NUMS:
                    dve.wait_ge(num_split, n - NUMS + 1)
                parts = []
                split_at = turned(g, j) * P
                if split_at > 0:
                    dve.wait_ge(sim_ready, n + 1)
                    parts.append((psS[:, j % 2, :], slice(0, split_at)))
                if split_at < GR:
                    dve.wait_ge(exp_ready, exp_no(g, j))
                    parts.append((exp_of(j), slice(split_at, GR)))
                for e, cols in parts:
                    last = nc.vector.scalar_tensor_tensor(nums[:, n % NUMS, cols], adj[:, (j // GB) % 2, j % GB, cols],
                                                          ADJ_EPS, e[:, cols], ALU.add, ALU.mult)
                last.then_inc(num_ready, 1)

            def lo_of_numerators(g, j):
                n = g * NB + j
                dve.wait_ge(num_hi, n + 1)
                nc.vector.scalar_tensor_tensor(alo[:, (j // GB) % 2, j % GB, :], nums[:, n % NUMS, :], P_SCALE,
                                               ahi[:, (j // GB) % 2, j % GB, :], ALU.mult, ALU.subtract)\
                    .then_inc(num_split, 1)

            def att_group(g, tp, tg):
                for j in range(NB):
                    numerators(g, j)
                    if j > 0:
                        lo_of_numerators(g, j - 1)
                    elif g > 0:
                        lo_of_numerators(g - 1, NB - 1)
                    for name in ATT_PLACES[g > 0].get(j, []):
                        stage(name, tp, tg)

            def lo_of_weights(part, n):
                dve.wait_ge(w_hi, n)
                nc.vector.scalar_tensor_tensor(wsp[:, 1, part], shared[:, part], W_SCALE, wsp[:, 0, part],
                                               ALU.mult, ALU.subtract).then_inc(w_ready, 1)

            for name in ["stats", "norm", "h"]:
                stage(name, PRE, 0)
            lo_of_weights(slice(0, wofs[1]), 1)
            stage("stats", PRE, 1)
            split(0, 0, 0)
            for q in range(NG):
                if q + 1 < NG:
                    stage("norm", PRE, q + 1)
                if q > 0:
                    stage("W0", PRE, q)
                if q + 1 < NG:
                    stage("h", PRE, q + 1)
                if q == 0:
                    stage("W0", PRE, q)
                stage("W1", PRE, q)
                if q + 2 < NG:
                    stage("stats", PRE, q + 2)
                if q != 1:
                    split(0, 0, max(1, q))
            lo_of_weights(slice(wofs[1], wofs[5]), 2)
            dve.wait_ge(diag_loaded, 16 * GB)
            nc.vector.tensor_scalar(diag[:, :], diag[:, :], 1.0, None, ALU.add).then_inc(diag_one, 1)
            dve.wait_ge(b_loaded, 32)
            for p in range(6):
                if p == ATT:
                    dve.wait_ge(dinv_ready, 2 * NG)
                    for g in range(NG):
                        att_group(g, *((ATT, g - 1) if g else (1, NG - 1)))
                    lo_of_numerators(NG - 1, NB - 1)
                else:
                    if p > 0:
                        group(p, 0, p - 1, NG - 1)
                    with dve.Fori(1, NG) as g:
                        group(p, g, p, g - 1)
            dve.wait_ge(direct_ready, at(DIRECT, 4, NG - 1, GB, GB))
            for b in range(GB):
                j = (NG - 1) * GB + b
                add_cross(5, NG - 1, b)
                dve.wait_ge(ev_ready, at(ALL, 5, NG - 1, GB, b + 1))
                nc.vector.tensor_tensor(o[:, b, :], o[:, b, :], direct[:, j, :], ALU.add).then_inc(preact, 1)
                dve.wait_ge(preact, at([5], 5, NG - 1, 1, b + 1))
                nc.vector.scalar_tensor_tensor(xres[:, j, :], o[:, b, :], 0.0, xres[:, j, :], ALU.max, ALU.add)\
                    .then_inc(x_ready, 1)


def kernel(x, adj, L0_gnn_W, L1_gnn_weight, L1_gnn_bias, L2_gnn_W, L2_gnn_b, L3_gnn_W1, L3_gnn_W2):
    import concourse.bacc as bacc
    from concourse.bass_utils import run_bass_kernel_spmd

    def rows_on_partitions(w):
        return w.reshape(-1, P, w.shape[1]).transpose(1, 0, 2)

    def halves(w):
        return rows_on_partitions(np.concatenate([w[:F], w[F:]], axis=1))

    arrays = {
        "x": np.asarray(x).reshape(NG, GB, P, F).transpose(0, 2, 1, 3).reshape(NG * P, GB * F),
        "adj_t": np.asarray(adj).reshape(NG, GR, NC, GB, P).transpose(0, 2, 4, 3, 1).reshape(NG * NC * P, GB * GR),
        "w0": rows_on_partitions(np.asarray(L0_gnn_W).T),
        "wg": rows_on_partitions(np.asarray(L1_gnn_weight)),
        "bias_g": np.asarray(L1_gnn_bias).reshape(1, F),
        "w2": rows_on_partitions(np.asarray(L2_gnn_W)),
        "bias_2": np.asarray(L2_gnn_b).reshape(1, F),
        "w3a": halves(np.asarray(L3_gnn_W1)),
        "w3b": halves(np.asarray(L3_gnn_W2)),
    }
    nc = bacc.Bacc("TRN2", target_bir_lowering=False, num_devices=1, dynamic_dma_scratch_size=1024)
    aps = {}
    for name, a in arrays.items():
        arrays[name] = np.ascontiguousarray(a)
        aps[name] = nc.dram_tensor(f"in_{name}", a.shape, mybir.dt.from_np(a.dtype), kind="ExternalInput").ap()
    out = nc.dram_tensor("out", (N, F), mybir.dt.float32, kind="ExternalOutput").ap()
    sent = nc.dram_tensor("sent", (NC * (NC - 1) * P, 2 * GR), mybir.dt.float32, kind="Internal").ap()
    build(nc, sent=sent, out=out, **aps)
    r = run_bass_kernel_spmd(nc, [{f"in_{name}": a for name, a in arrays.items()}], core_ids=[0])
    return r.results[0]["out"]
```
